# Optimizing a Trainium2 kernel written in Bass

```python
import numpy as np
import jax
import jax.numpy as jnp

def _softmax(x, axis=-1):
    return jax.nn.softmax(x, axis=axis)

def _gelu(x):
    return jax.nn.gelu(x, approximate=True)

def _silu(x):
    return jax.nn.silu(x)

def _sigmoid(x):
    return jax.nn.sigmoid(x)

def _layernorm(x, axis=-1, eps=1e-05):
    m = jnp.mean(x, axis=axis, keepdims=True)
    v = jnp.var(x, axis=axis, keepdims=True)
    return (x - m) / jnp.sqrt(v + eps)

def _scatter_add(tgt, idx, src, axis=0):
    return tgt.at[idx].add(src)

def _segment_sum(src, seg, n):
    return jax.ops.segment_sum(src, seg, n)
kernel_name = 'mk_prb_d1_jaxref_r8_5c19c8'

def setup_inputs(seed: int=0):
    np.random.seed(seed)
    _w = jnp.asarray

    def _L0_attn_setup():
        import jax, jax.numpy as jnp
        import numpy as np
        D_MODEL = 256
        N_HEADS = 16
        HEAD_DIM = D_MODEL // N_HEADS
        B, T = (2, 256)
        key = jax.random.key(seed)
        ks = jax.random.split(key, 9)
        s = 0.02
        x = jax.random.normal(ks[0], (B, T, D_MODEL), dtype=jnp.float32)
        Wq = jax.random.normal(ks[1], (N_HEADS, D_MODEL, HEAD_DIM), dtype=jnp.float32) * s
        bq = jax.random.normal(ks[2], (N_HEADS, HEAD_DIM), dtype=jnp.float32) * s
        Wk = jax.random.normal(ks[3], (N_HEADS, D_MODEL, HEAD_DIM), dtype=jnp.float32) * s
        bk = jax.random.normal(ks[4], (N_HEADS, HEAD_DIM), dtype=jnp.float32) * s
        Wv = jax.random.normal(ks[5], (N_HEADS, D_MODEL, HEAD_DIM), dtype=jnp.float32) * s
        bv = jax.random.normal(ks[6], (N_HEADS, HEAD_DIM), dtype=jnp.float32) * s
        Wo = jax.random.normal(ks[7], (D_MODEL, D_MODEL), dtype=jnp.float32) * s
        bo = jax.random.normal(ks[8], (D_MODEL,), dtype=jnp.float32) * s
        return {'x': x, 'Wq': Wq, 'bq': bq, 'Wk': Wk, 'bk': bk, 'Wv': Wv, 'bv': bv, 'Wo': Wo, 'bo': bo}
    _L0_attn_in = _L0_attn_setup()

    def _L0_ffn_setup():
        import jax, jax.numpy as jnp
        import numpy as np
        NUM_EXPERTS = 8
        TOP_K = 2
        HIDDEN = 256
        INTER = 256
        SWIGLU_LIMIT = 7.0
        BATCH, SEQ = (4, 256)
        key = jax.random.key(seed)
        k0, k1, k2, k3, k4 = jax.random.split(key, 5)
        x = jax.random.normal(k0, (BATCH, SEQ, HIDDEN), jnp.float32)
        Wr = jax.random.normal(k1, (HIDDEN, NUM_EXPERTS), jnp.float32) * 0.02
        Wg = jax.random.normal(k2, (NUM_EXPERTS, HIDDEN, INTER), jnp.float32) * 0.02
        Wu = jax.random.normal(k3, (NUM_EXPERTS, HIDDEN, INTER), jnp.float32) * 0.02
        Wd = jax.random.normal(k4, (NUM_EXPERTS, INTER, HIDDEN), jnp.float32) * 0.02
        return {'hidden_states': x, 'Wr': Wr, 'Wg': Wg, 'Wu': Wu, 'Wd': Wd}
    _L0_ffn_in = _L0_ffn_setup()
    _d = {'L0_attn_x': _L0_attn_in['x'], 'L0_attn_Wq': _L0_attn_in['Wq'], 'L0_attn_bq': _L0_attn_in['bq'], 'L0_attn_Wk': _L0_attn_in['Wk'], 'L0_attn_bk': _L0_attn_in['bk'], 'L0_attn_Wv': _L0_attn_in['Wv'], 'L0_attn_bv': _L0_attn_in['bv'], 'L0_attn_Wo': _L0_attn_in['Wo'], 'L0_attn_bo': _L0_attn_in['bo'], 'L0_ffn_Wr': _L0_ffn_in['Wr'], 'L0_ffn_Wg': _L0_ffn_in['Wg'], 'L0_ffn_Wu': _L0_ffn_in['Wu'], 'L0_ffn_Wd': _L0_ffn_in['Wd']}
    _x0 = _d['L0_attn_x']
    _d['L0_attn_x'] = jax.random.normal(jax.random.fold_in(jax.random.key(seed), 1), (2, 1024, 256), dtype=_x0.dtype)
    del _x0
    return _d

def reference(L0_attn_x, L0_attn_Wq, L0_attn_bq, L0_attn_Wk, L0_attn_bk, L0_attn_Wv, L0_attn_bv, L0_attn_Wo, L0_attn_bo, L0_ffn_Wr, L0_ffn_Wg, L0_ffn_Wu, L0_ffn_Wd):

    def _L0_attn_ref(x, Wq, bq, Wk, bk, Wv, bv, Wo, bo):
        import jax, jax.numpy as jnp
        import numpy as np
        D_MODEL = 256
        N_HEADS = 16
        HEAD_DIM = D_MODEL // N_HEADS
        B, T = (2, 256)
        Bn, Tn, C = x.shape
        H, _, D = Wq.shape
        scale = D ** (-0.5)
        q = jnp.einsum('btc,hcd->bhtd', x, Wq) + bq[None, :, None, :]
        k = jnp.einsum('btc,hcd->bhtd', x, Wk) + bk[None, :, None, :]
        v = jnp.einsum('btc,hcd->bhtd', x, Wv) + bv[None, :, None, :]
        scores = jnp.einsum('bhtd,bhsd->bhts', q, k) * scale
        neg = jnp.finfo(scores.dtype).min
        causal = jnp.triu(jnp.full((Tn, Tn), neg, dtype=scores.dtype), k=1)
        probs = jax.nn.softmax(scores + causal, axis=-1)
        y = jnp.einsum('bhts,bhsd->bhtd', probs, v)
        y = y.transpose(0, 2, 1, 3).reshape(Bn, Tn, H * D)
        return y @ Wo + bo

    def _L0_ffn_ref(hidden_states, Wr, Wg, Wu, Wd):
        import jax, jax.numpy as jnp
        import numpy as np
        NUM_EXPERTS = 8
        TOP_K = 2
        HIDDEN = 256
        INTER = 256
        SWIGLU_LIMIT = 7.0
        BATCH, SEQ = (4, 256)
        router_logits = jnp.einsum('bsh,he->bse', hidden_states, Wr)
        topk_logits, selected = jax.lax.top_k(router_logits, TOP_K)
        router_probs = jax.nn.softmax(topk_logits, axis=-1)
        out = jnp.zeros_like(hidden_states)
        for e in range(NUM_EXPERTS):
            w_e = jnp.where(selected == e, router_probs, 0.0).sum(axis=-1, keepdims=True)
            g = jnp.einsum('bsh,hi->bsi', hidden_states, Wg[e])
            g = jnp.clip(jax.nn.silu(g), -SWIGLU_LIMIT, SWIGLU_LIMIT)
            u = jnp.einsum('bsh,hi->bsi', hidden_states, Wu[e])
            h = jnp.einsum('bsi,ih->bsh', g * u, Wd[e])
            out = out + h * w_e
        return out
    x = L0_attn_x
    xn = _layernorm(x, axis=-1)
    x = x + _L0_attn_ref(xn, L0_attn_Wq, L0_attn_bq, L0_attn_Wk, L0_attn_bk, L0_attn_Wv, L0_attn_bv, L0_attn_Wo, L0_attn_bo) + _L0_ffn_ref(xn, L0_ffn_Wr, L0_ffn_Wg, L0_ffn_Wu, L0_ffn_Wd)
    return x

_drawn_inputs = setup_inputs


def setup_inputs(seed=0):
    import zlib

    import numpy as np

    out = dict(_drawn_inputs(seed))
    spreads = {}
    factors = {'L0_attn_Wq': 8.0,
     'L0_attn_bq': 8.0,
     'L0_attn_Wk': 8.0,
     'L0_attn_bk': 64.0,
     'L0_attn_Wv': 6.421,
     'L0_attn_bv': 8.0,
     'L0_attn_Wo': 5.035,
     'L0_attn_bo': 9.348,
     'L0_ffn_Wr': 5.46,
     'L0_ffn_Wg': 4.738,
     'L0_ffn_Wu': 4.684,
     'L0_ffn_Wd': 4.687}
    for name, (base, spread) in spreads.items():
        noise = np.random.default_rng([zlib.crc32(name.encode()), seed]).standard_normal(out[name].shape)
        drawn = base * np.exp(spread * noise) if base else spread * noise
        out[name] = jnp.asarray(drawn.astype(out[name].dtype))
    for name, factor in factors.items():
        out[name] = (out[name] * factor).astype(out[name].dtype)
    return out
```

```python
from contextlib import ExitStack

import concourse.bass as bass
import numpy as np
from concourse import mybir

F32 = mybir.dt.float32
BF16 = mybir.dt.bfloat16
I32 = mybir.dt.int32
U32 = mybir.dt.uint32
ALU = mybir.AluOpType
ACT = mybir.ActivationFunctionType
AX = mybir.AxisListType

P = 128
B, T, D = 2, 1024, 256
H, HD = 16, 16
E, F = 8, 256
N = B * T
NT = N // P
TB = T // P
DC = D // P
EPS = 1e-5
SCALE = HD ** -0.5
LIMIT = 7.0
NEG = -3.0e38
BANK = 512

UH = 4
G = H // UH
UNITS = B * G
PARTS = 3
Q_PARTS = (0, 1, 2, 0, 1, 0)
K_PARTS = (0, 0, 0, 1, 1, 2)
MAXROW = HD * len(Q_PARTS)
KROWS = MAXROW + PARTS
SLOTS = 3
VW = HD + 1
VROW = H * VW + 32 - VW
STEPS = [(c, j) for c in range(T // BANK) for j in range((c + 1) * BANK // P)]
NS = len(STEPS)
CHUNKS = [(h, i, s) for h in range(UH) for i in range(TB) for s in range(i * P // BANK + 1)]
NCH = len(CHUNKS)
CH_PER_STEP = 5
QKS = B * 2 * (H * HD // P) * (T // BANK)

MAX_TILES = 2 * N // P + E - 1
PAD = 4 * N


CONSTS = 6


def step_span(n):
    c, j = STEPS[n]
    t0 = max(P * j, BANK * c)
    return t0, BANK * (c + 1) - t0


def diagonal(n):
    c, j = STEPS[n]
    return P * j >= BANK * c


DIAG = [sum(diagonal(m) for m in range(n)) for n in range(NS + 1)]


def build(nc, x_d, wqk_d, wvr_d, bqk_d, bv_d, wo_d, bo_d, wgu_d, wd_d, out_d):
    with ExitStack() as ctx:
        def sb(name, shape, dt=F32):
            return ctx.enter_context(nc.sbuf_tensor(name, shape, dt))

        def sem(name):
            return ctx.enter_context(nc.semaphore(name))

        xn_d = nc.dram_tensor("xn_rows", [N, D], F32).ap()
        qk_d = nc.dram_tensor("qk_parts", [2, PARTS, H, HD, N], BF16).ap()
        slot_d = nc.dram_tensor("slot_values", [MAX_TILES * P, 1], I32).ap()
        z_d = nc.dram_tensor("expert_rows", [2 * N, D], F32).ap()

        x = sb("x", [P, NT, D])
        xnt_moe = sb("xnt", [P, DC, N])
        wqk = sb("wqk", [P, 2, DC, H * HD])
        wvr = sb("wvr", [P, DC, H * HD + E])
        wo = sb("wo", [P, DC, D])
        bqk = sb("bqk", [P, 2, 2])
        bv = sb("bv", [P, H * HD])
        bo = sb("bo", [P, D])
        stats = sb("stats", [P, NT, 6])
        mv = sb("mv", [P, NT, 2])
        vareps = sb("vareps", [P, NT])
        rstd = sb("rstd", [P, NT])
        neghalf = sb("neghalf", [P, 4])
        stage = sb("stage", [P, 2, PARTS, T], BF16)
        resid = sb("resid", [P, 2, BANK])
        v = sb("v", [P, NT, VROW])
        packq = sb("packq", [P, SLOTS, UH, T], BF16)
        packk = sb("packk", [P, SLOTS, UH, T], BF16)
        probs = sb("probs", [P, 2, UH, BANK])
        xn = probs[:, :, :, :].rearrange("p a h n -> p (a h n)").rearrange("p (t d) -> p t d", d=D)
        maskrow = sb("maskrow", [P, BANK], BF16)
        junk = sb("junk", [P, 2, BANK], BF16)
        mxa = sb("mxa", [P, 2, UH, TB])
        mxb = sb("mxb", [P, 2, UH, TB // 2])
        negm = sb("negm", [P, PARTS, UH, TB], BF16)
        negr = sb("negr", [P, UH, TB])
        negt = sb("negt", [P, P], BF16)
        yraw = resid[:, 0, :]
        rec = sb("rec", [P, 4, UH])
        y = sb("y", [P, TB, D])
        yt = sb("yt", [P, 4, P])
        ident = sb("ident", [P, P])
        identb = sb("identb", [P, P], BF16)
        lower = sb("lower", [P, P], BF16)
        ones = sb("ones", [P, P], BF16)
        iota8 = sb("iota8", [P, E])
        iota128 = sb("iota128", [P, NT])
        iota_t = sb("iota_t", [P, MAX_TILES])
        slot_val = sb("slot_val", [P, NT, 2], I32)
        padv = sb("padv", [P, MAX_TILES], I32)
        lg = sb("lg", [P, NT, E])
        top = sb("top", [P, NT, E])
        topi = sb("topi", [P, NT, E], U32)
        topf = sb("topf", [P, NT, 2])
        dl = sb("dl", [P, NT])
        eg = sb("eg", [P, NT])
        gate = sb("gate", [P, NT, 2])
        hot = sb("hot", [P, 2, NT, E], BF16)
        hots = sb("hots", [P, NT, E], BF16)
        fits = sb("fits", [P, E, NT])
        ntile = sb("ntile", [P, E])
        tend = sb("tend", [P, E])
        one8 = sb("one8", [P, E])
        sbase = sb("sbase", [P, E])
        place = sb("place", [P, NT, E])
        prod = sb("prod", [P, 2, NT, E])
        posf = sb("posf", [P, 2, NT])
        posi = sb("posi", [P, 2, NT], I32)
        postile = sb("postile", [P, 2, NT], I32)
        posrow = sb("posrow", [P, 2, NT], I32)
        pos = sb("pos", [P, 2, NT], U32)
        below = sb("below", [P, MAX_TILES, E])
        eidf = sb("eidf", [P, MAX_TILES])
        eid = sb("eid", [P, MAX_TILES], I32)
        slots = sb("slots", [P, MAX_TILES], I32)
        clip = sb("clip", [P, MAX_TILES], I32)
        token = sb("token", [P, MAX_TILES], I32)
        wgu = sb("wgu", [P, E * DC * 2 * F])
        wd = xnt_moe[:, :, :].rearrange("p c n -> p (c n)")
        xg = sb("xg", [P, 2, D])
        xgt = sb("xgt", [P, 2, DC, P])
        silu = sb("silu", [P, 2, F])
        hid = sb("hid", [P, 2, F])
        hidt = sb("hidt", [P, 2, DC, P])
        yo = sb("yo", [P, 2, D])
        z = stage[:, :, :, :].rearrange("p a b t -> p (a b t)").bitcast(F32)[:, 0:2 * 2 * 2 * D // 2]
        z = z.rearrange("p (r k d) -> p r k d", r=2, k=2)

        ps_s = ctx.enter_context(nc.psum_tensor("ps_s", [P, UH, BANK], F32))
        ps_m = ctx.enter_context(nc.psum_tensor("ps_m", [P, 2, BANK], F32))
        ps_y = ctx.enter_context(nc.psum_tensor("ps_y", [P, BANK], F32))
        ps_t = ctx.enter_context(nc.psum_tensor("ps_t", [P, BANK], F32))

        x_in = [sem(f"x_in{q}") for q in range(4)]
        w_in = sem("w_in")
        wgu_in = sem("wgu_in")
        wd_in = sem("wd_in")
        consts = sem("consts")
        const_step = sem("const_step")
        ln_step = sem("ln_step")
        var_ready = sem("var_ready")
        rstd_ready = sem("rstd_ready")
        xn_ready = sem("xn_ready")
        xn_out = sem("xn_out")
        xnt_raw = sem("xnt_raw")
        xnt_ready = sem("xnt_ready")
        qk_raw = sem("qk_raw")
        qk_hi = sem("qk_hi")
        qk_resid = sem("qk_resid")
        qk_mid = sem("qk_mid")
        qk_lo = sem("qk_lo")
        qk_out = [sem(f"qk_out{i}") for i in range(2)]
        v_raw = sem("v_raw")
        v_ready = sem("v_ready")
        pack_in = [sem(f"pack_in{i}") for i in range(SLOTS)]
        maxrow_zero = sem("maxrow_zero")
        nat_ready = sem("nat_ready")
        max_done = sem("max_done")
        neg_step = sem("neg_step")
        neg_cols = sem("neg_cols")
        neg_in = [sem(f"neg_in{i}") for i in range(SLOTS)]
        tr_ready = sem("tr_ready")
        tr_free = sem("tr_free")
        scores_ready = sem("scores_ready")
        probs_ready = sem("probs_ready")
        probs_masked = sem("probs_masked")
        pv_done = sem("pv_done")
        y_raw = sem("y_raw")
        rec_ready = sem("rec_ready")
        y_ready = sem("y_ready")
        yt_raw = sem("yt_raw")
        yt_ready = sem("yt_ready")
        proj_raw = sem("proj_raw")
        proj_done = sem("proj_done")
        route_step = sem("route_step")
        gate_logit = sem("gate_logit")
        gate_exp = sem("gate_exp")
        hots_ready = sem("hots_ready")
        pos_ready = sem("pos_ready")
        list_init = sem("list_init")
        list_out = sem("list_out")
        list_in = sem("list_in")
        eid_ready = sem("eid_ready")
        token_ready = sem("token_ready")
        gather_in = [sem(f"gather_in{i}") for i in range(2)]
        xgt_raw = sem("xgt_raw")
        xgt_ready = sem("xgt_ready")
        gu_raw = sem("gu_raw")
        silu_ready = sem("silu_ready")
        hid_ready = sem("hid_ready")
        hidt_raw = sem("hidt_raw")
        hidt_ready = sem("hidt_ready")
        yo_raw = sem("yo_raw")
        yo_ready = sem("yo_ready")
        scatter_out = [sem(f"scatter_out{i}") for i in range(2)]
        z_in = [sem(f"z_in{i}") for i in range(2)]
        sum_step = sem("sum_step")
        out_ready = sem("out_ready")
        out_done = sem("out_done")

        tr_order = [("route",), ("neg", 0)]
        for u in range(UNITS):
            tr_order += [("y", u, 0)] + ([("neg", u + 1)] if u + 1 < UNITS else []) + [("y", u, 1)]
        tr_at = {k: n for n, k in enumerate(tr_order)}

        def pack_dmas(u):
            b, g = divmod(u, G)
            heads, cols = slice(UH * g, UH * g + UH), slice(T * b, T * b + T)
            for op, (pack, parts) in enumerate(((packq, Q_PARTS), (packk, K_PARTS))):
                for r, part in enumerate(parts):
                    yield (pack[HD * r:HD * r + HD, u % SLOTS, :, :],
                           qk_d[op, part, heads, :, cols].rearrange("h d t -> d h t"))

        PACKS = 2 * len(Q_PARTS)

        def span_rows(q):
            return slice(4 * q, 4 * q + 4)

        block = ctx.enter_context(nc.Block())

        @block.sync
        def _(sp):
            for q in range(4):
                sp.dma_start(x[:, span_rows(q), :],
                             x_d[P * 4 * q:P * 4 * (q + 1), :].rearrange("(t p) d -> p t d", p=P)).then_inc(x_in[q], 16)
            sp.wait_ge(consts, 1)
            sp.dma_start(slot_d.rearrange("(p c) o -> p (c o)", p=P), padv[:, :]).then_inc(list_init, 16)
            for q in range(4):
                sp.wait_ge(xn_ready, 4 * (q + 1))
                sp.dma_start(xn_d[P * 4 * q:P * 4 * (q + 1), :].rearrange("(t p) d -> p t d", p=P),
                             xn[:, span_rows(q), :]).then_inc(xn_out, 16)

            def store_parts(w):
                b, r = divmod(w, 4)
                op, grp = divmod(r, 2)
                sp.wait_ge(qk_hi, 2 * w + 2)
                sp.wait_ge(qk_mid, 2 * w + 2)
                sp.wait_ge(qk_lo, 2 * w + 2)
                for part in range(PARTS):
                    dst = qk_d[op, part, 8 * grp:8 * grp + 8, :, T * b:T * b + T].rearrange("h d t -> (h d) t")
                    sp.dma_start(dst, stage[:, w % 2, part, :]).then_inc(qk_out[w % 2], 16)

            def load_unit(u):
                if u >= SLOTS:
                    sp.wait_ge(scores_ready, 2 * NS * (u - SLOTS + 1))
                for s in qk_out:
                    sp.wait_ge(s, 2 * 16 * PARTS * (u // G + 1))
                for dst, src in pack_dmas(u):
                    sp.dma_start(dst, src).then_inc(pack_in[u % SLOTS], 16)

            def neg_dmas(u):
                sp.wait_ge(tr_free, tr_at[("neg", u)] + 1)
                for part in range(PARTS):
                    dst = packq[MAXROW + part:MAXROW + part + 1, u % SLOTS, :, :]
                    sp.dma_start(dst.rearrange("o h (i t) -> o (h i) t", t=P),
                                 negt[32 * part:32 * part + 32, :]).then_inc(neg_in[u % SLOTS], 16)

            def load_z(i):
                if i >= 2:
                    sp.wait_ge(out_ready, i - 1)
                sp.dma_start(z[:, i % 2, :, :],
                             z_d[2 * P * i:2 * P * (i + 1), :].rearrange("(p k) d -> p k d", k=2)).then_inc(z_in[i % 2], 16)

            def store_out(i):
                sp.wait_ge(out_ready, i + 1)
                sp.dma_start(out_d[P * i:P * (i + 1), :], x[:, i, :]).then_inc(out_done, 16)

            for w in range(4):
                store_parts(w)
            load_unit(0)
            load_unit(1)
            for w in range(4, 8):
                store_parts(w)
            load_unit(2)
            neg_dmas(0)
            sp.wait_ge(v_raw, NT)
            sp.wait_ge(qk_raw, QKS)
            sp.dma_start(wd, wd_d).then_inc(wd_in, 16)
            for u in range(UNITS):
                if u + 1 < UNITS:
                    neg_dmas(u + 1)
                if u + SLOTS < UNITS:
                    load_unit(u + SLOTS)
                if u == 1:
                    sp.wait_ge(list_out, 16 * 2 * NT)
                    sp.dma_start(slots[:, :], slot_d.rearrange("(p i) o -> p (i o)", p=P)).then_inc(list_in, 16)
                if u == G - 1:
                    for s in range(2):
                        sp.wait_ge(scatter_out[s], 16 * len(range(s, MAX_TILES, 2)))
                    load_z(0)
                    load_z(1)
                if u >= G:
                    for i in (2 * (u - G), 2 * (u - G) + 1):
                        store_out(i)
                        load_z(i + 2)
            for i in range(TB, NT):
                store_out(i)
                if i + 2 < NT:
                    load_z(i + 2)
            sp.wait_ge(out_done, 16 * NT)
            sp.wait_ge(xn_out, 16 * 4)

        @block.gpsimd
        def _(pool):
            steps = [0]

            def chain(ins):
                ins.then_inc(const_step, 1)
                steps[0] += 1
                pool.wait_ge(const_step, steps[0])

            def inverse_deviation(q):
                pool.wait_ge(var_ready, q + 1)
                pool.tensor_tensor(rstd[:, span_rows(q)], vareps[:, span_rows(q)], neghalf[:, :], ALU.pow)\
                    .then_inc(rstd_ready, 1)

            pool.memset(padv[:, :], PAD).then_inc(consts, 1)
            chain(pool.memset(neghalf[:, :], -0.5))
            chain(pool.memset(ident[:, :], 0.0))
            chain(pool.affine_select(out=ident[:, :], in_=ident[:, :], compare_op=ALU.not_equal, fill=1.0, base=0,
                                     pattern=[[-1, P]], channel_multiplier=1))
            pool.tensor_copy(identb[:, :], ident[:, :]).then_inc(consts, 1)
            inverse_deviation(0)
            chain(pool.memset(maskrow[:, :], 0.0))
            pool.affine_select(out=maskrow[:, BANK - P:], in_=maskrow[:, BANK - P:], compare_op=ALU.is_ge, fill=NEG,
                               base=0, pattern=[[-1, P]], channel_multiplier=1).then_inc(consts, 1)
            inverse_deviation(1)
            chain(pool.memset(lower[:, :], 0.0))
            pool.affine_select(out=lower[:, :], in_=lower[:, :], compare_op=ALU.is_ge, fill=1.0, base=0,
                               pattern=[[-1, P]], channel_multiplier=1).then_inc(consts, 1)
            inverse_deviation(2)
            pool.memset(one8[:, :], 1.0)
            pool.iota(iota8[:, :], pattern=[[1, E]], base=0, channel_multiplier=0, allow_small_or_imprecise_dtypes=True)
            pool.iota(iota128[:, :], pattern=[[P, NT]], base=0, channel_multiplier=0,
                      allow_small_or_imprecise_dtypes=True)
            inverse_deviation(3)
            pool.iota(iota_t[:, :], pattern=[[1, MAX_TILES]], base=0, channel_multiplier=0,
                      allow_small_or_imprecise_dtypes=True)
            pool.iota(slot_val[:, :, :], pattern=[[2 * P, NT], [1, 2]], base=0, channel_multiplier=2).then_inc(consts, 1)
            chain(pool.memset(v[:, :, :], 1.0))
            chain(pool.memset(packq[MAXROW:KROWS, :, :, :], 0.0))
            chain(pool.memset(packk[MAXROW:KROWS, :, :, :], 1.0))
            pool.memset(ones[:, :], 1.0).then_inc(consts, 1)

            def place_tokens(i):
                for k in range(2):
                    pool.indirect_dma_start(out=slot_d, out_offset=bass.IndirectOffsetOnAxis(ap=pos[:, k, i:i + 1], axis=0),
                                            in_=slot_val[:, i, k:k + 1], in_offset=None).then_inc(list_out, 16)

            def gather(i):
                if i >= 2:
                    pool.wait_ge(xgt_raw, i - 1)
                pool.indirect_dma_start(out=xg[:, i % 2, :], out_offset=None, in_=xn_d,
                                        in_offset=bass.IndirectOffsetOnAxis(ap=token[:, i:i + 1], axis=0))\
                    .then_inc(gather_in[i % 2], 16)

            def scatter(i):
                pool.wait_ge(yo_ready, i + 1)
                pool.indirect_dma_start(out=z_d, out_offset=bass.IndirectOffsetOnAxis(ap=slots[:, i:i + 1], axis=0),
                                        in_=yo[:, i % 2, :], in_offset=None, bounds_check=2 * N - 1, oob_is_err=False)\
                    .then_inc(scatter_out[i % 2], 16)

            for u in range(UNITS):
                if u >= SLOTS:
                    pass
                for n in range(NS):
                    g = NS * u + n
                    if diagonal(n):
                        pool.wait_ge(probs_ready, 2 * g + 2)
                        cols = probs[:, g % 2, :, 0:P]
                        pool.affine_select(out=cols, in_=cols, compare_op=ALU.is_ge, fill=0.0, base=0,
                                           pattern=[[0, UH], [1, P]], channel_multiplier=-1).then_inc(probs_masked, 1)
                    if u == 0 and n == 0:
                        pool.wait_ge(pos_ready, 1)
                        pool.wait_ge(list_init, 16)
                    if u < 2 and n < 8:
                        place_tokens(8 * u + n)
                    if n == 0 and u + 2 >= SLOTS and u + 2 < UNITS:
                        pool.wait_ge(scores_ready, 2 * NS * (u + 2 - SLOTS + 1))
                        pool.wait_ge(probs_masked, DIAG[NS] * u + 1)
                        pool.memset(packq[MAXROW:KROWS, (u + 2) % SLOTS, :, :], 0.0).then_inc(maxrow_zero, 1)
                        pool.wait_ge(maxrow_zero, u + 2 - SLOTS + 1)
                if u == G - 1:
                    pool.wait_ge(token_ready, 1)
                    pool.wait_ge(xn_out, 16 * 4)
                    gather(0)
                    gather(1)
                    for i in range(MAX_TILES):
                        if i + 2 < MAX_TILES:
                            gather(i + 2)
                        scatter(i)

        @block.scalar
        def _(act):
            for dst, src in ((wqk[:, :, :, :], wqk_d), (wvr[:, :, :], wvr_d), (wo[:, :, :], wo_d), (bqk[:, :, :], bqk_d),
                             (bv[:, :], bv_d.partition_broadcast(P)), (bo[:, :], bo_d.partition_broadcast(P))):
                act.dma_start(dst, src).then_inc(w_in, 16)
            act.dma_start(wgu[:, :], wgu_d).then_inc(wgu_in, 16)

            def evacuate_xnt(r):
                q, c = divmod(r, DC)
                act.wait_ge(xnt_raw, r + 1)
                act.copy(xnt_moe[:, c, 4 * P * q:4 * P * (q + 1)], ps_s[:, r % 4, :]).then_inc(xnt_ready, 1)

            def qk_hi_part(k):
                w, n = divmod(k, 2)
                op, grp = divmod(w % 4, 2)
                if k == 0:
                    act.wait_ge(w_in, 16 * 6)
                act.wait_ge(qk_raw, k + 1)
                if w >= 2:
                    act.wait_ge(qk_out[w % 2], 16 * PARTS * (w // 2))
                act.activation(stage[:, w % 2, 0, BANK * n:BANK * (n + 1)], ps_s[:, k % 4, :], ACT.Identity,
                               bias=bqk[:, op, grp:grp + 1], scale=1.0).then_inc(qk_hi, 1)

            def qk_mid_part(k):
                w, n = divmod(k, 2)
                act.wait_ge(qk_resid, k + 1)
                act.copy(stage[:, w % 2, 1, BANK * n:BANK * (n + 1)], resid[:, k % 2, :]).then_inc(qk_mid, 1)

            for r in range(4):
                evacuate_xnt(r)
            for k in range(QKS // 2):
                qk_hi_part(k)
                if k:
                    qk_mid_part(k - 1)
            qk_mid_part(QKS // 2 - 1)
            for r in range(4, 8):
                evacuate_xnt(r)
            for k in range(QKS // 2, QKS):
                qk_hi_part(k)
                if k > QKS // 2:
                    qk_mid_part(k - 1)
            qk_mid_part(QKS - 1)
            act.wait_ge(gate_logit, 1)
            act.activation(eg[:, :], dl[:, :], ACT.Exp).then_inc(gate_exp, 1)

            def copy_y(u, c):
                first = NS * u + (0 if c == 0 else 4)
                last = NS * u + (3 if c == 0 else NS - 1)
                act.wait_ge(pv_done, last + 1)
                if 2 * u + c >= 1:
                    uu, cc = divmod(2 * u + c - 1, 2)
                    act.wait_ge(tr_ready, tr_at[("y", uu, cc)] + 1)
                act.copy(yraw[:, :], ps_y[:, :]).then_inc(y_raw, 1)

            def project_copies(b):
                for w in range(TB // 2):
                    act.wait_ge(yt_raw, TB // 2 * b + w + 1)
                    if TB // 2 * b + w >= 1:
                        act.wait_ge(proj_raw, 2 * (TB // 2 * b + w))
                    act.copy(yt[:, :, :], ps_t[:, :].rearrange("p (a t) -> p a t", a=4)).then_inc(yt_ready, 1)

            def exps(g):
                _, width = step_span(g % NS)
                for pr in range(2):
                    act.wait_ge(scores_ready, 2 * g + pr + 1)
                    if g >= 2:
                        act.wait_ge(pv_done, g - 1)
                    act.activation(probs[:, g % 2, 2 * pr:2 * pr + 2, 0:width], ps_s[:, 2 * pr:2 * pr + 2, 0:width],
                                   ACT.Exp, scale=SCALE).then_inc(probs_ready, 1)

            act.wait_ge(xn_out, 16 * 4)
            for u in range(UNITS):
                for n in range(NS):
                    exps(NS * u + n)
                    if n == 4:
                        copy_y(u, 0)
                    if n == 0 and u and u != G:
                        copy_y(u - 1, 1)
                if u % G == G - 1:
                    copy_y(u, 1)
                    project_copies(u // G)
                if u == G - 1:
                    for i in range(MAX_TILES):
                        act.wait_ge(xgt_raw, i + 1)
                        if i >= 2:
                            act.wait_ge(gu_raw, i - 1)
                        act.copy(xgt[:, i % 2, :, :], ps_s[:, 2, 0:D].rearrange("p (c t) -> p c t", c=DC))\
                            .then_inc(xgt_ready, 1)
                        act.wait_ge(gu_raw, i + 1)
                        if i >= 2:
                            act.wait_ge(hid_ready, i - 1)
                        act.activation(silu[:, i % 2, :], ps_s[:, i % 2, 0:F], ACT.Silu).then_inc(silu_ready, 1)

        @block.vector
        def _(dve):
            count = {}

            def chain(s, ins):
                ins.then_inc(s, 1)
                count[s.name] = count.get(s.name, 0) + 1
                dve.wait_ge(s, count[s.name])

            for q in range(4):
                dve.wait_ge(x_in[q], 16)
                for t in range(4 * q, 4 * q + 4):
                    ins = dve.bn_stats(stats[:, t, :], x[:, t, :])
                chain(ln_step, ins)
                for t in range(4 * q, 4 * q + 4):
                    ins = dve.bn_aggr(mv[:, t, :], stats[:, t, :])
                chain(ln_step, ins)
                dve.tensor_scalar(vareps[:, span_rows(q)], mv[:, span_rows(q), 1], EPS, None, ALU.add).then_inc(var_ready, 1)
                dve.wait_ge(rstd_ready, q + 1)
                for t in range(4 * q, 4 * q + 4):
                    dve.tensor_scalar(xn[:, t, :], x[:, t, :], mv[:, t, 0:1], rstd[:, t:t + 1], ALU.subtract, ALU.mult)\
                       .then_inc(xn_ready, 1)

            def qk_parts(k):
                w, n = divmod(k, 2)
                op, grp = divmod(w % 4, 2)
                cols = slice(BANK * n, BANK * (n + 1))
                dve.wait_ge(qk_hi, k + 1)
                if k >= 2:
                    dve.wait_ge(qk_lo, k - 1)
                dve.scalar_tensor_tensor(resid[:, k % 2, :], ps_s[:, k % 4, :], bqk[:, op, grp:grp + 1],
                                         stage[:, w % 2, 0, cols], ALU.add, ALU.subtract).then_inc(qk_resid, 1)

            def qk_lo_part(k):
                w, n = divmod(k, 2)
                cols = slice(BANK * n, BANK * (n + 1))
                dve.wait_ge(qk_mid, k + 1)
                dve.tensor_tensor(stage[:, w % 2, 2, cols], resid[:, k % 2, :], stage[:, w % 2, 1, cols],
                                  ALU.subtract).then_inc(qk_lo, 1)

            def row_max(u, m):
                h, i, s = CHUNKS[m]
                n = NCH * u + m
                width = min(P * (i + 1) - BANK * s, BANK)
                into = mxa[:, u % 2, h, i:i + 1] if s == 0 else mxb[:, u % 2, h, i - TB // 2:i - TB // 2 + 1]
                dve.wait_ge(nat_ready, n + 1)
                if n >= 2:
                    dve.wait_ge(max_done, n - 1)
                if s == i * P // BANK:
                    ins = dve.tensor_tensor_reduce(out=junk[:, n % 2, 0:width], in0=ps_m[:, n % 2, 0:width],
                                                   in1=maskrow[:, BANK - width:], scale=1.0, scalar=NEG,
                                                   op0=ALU.add, op1=ALU.max, accum_out=into)
                else:
                    ins = dve.tensor_reduce(into, ps_m[:, n % 2, 0:width], op=ALU.max, axis=AX.X)
                ins.then_inc(max_done, 1)

            def negate_max(u):
                dve.wait_ge(max_done, NCH * (u + 1))
                m = mxa[:, u % 2, :, :]
                chain(neg_step, dve.tensor_tensor(m[:, :, TB // 2:], m[:, :, TB // 2:], mxb[:, u % 2, :, :], ALU.max))
                if u:
                    dve.wait_ge(tr_ready, tr_at[("neg", u - 1)] + 1)
                chain(neg_step, dve.tensor_scalar(negm[:, 0, :, :], m, -1.0, None, ALU.mult))
                chain(neg_step, dve.scalar_tensor_tensor(negr[:, :, :], m, -1.0, negm[:, 0, :, :], ALU.mult, ALU.subtract))
                chain(neg_step, dve.tensor_copy(negm[:, 1, :, :], negr[:, :, :]))
                dve.tensor_tensor(negm[:, 2, :, :], negr[:, :, :], negm[:, 1, :, :], ALU.subtract).then_inc(neg_cols, 1)

            def copy_neg(u):
                n = tr_at[("neg", u)]
                dve.wait_ge(tr_ready, n + 1)
                if u:
                    dve.wait_ge(neg_in[(u - 1) % SLOTS], 16 * PARTS * ((u - 1) // SLOTS + 1))
                dve.tensor_copy(negt[0:96, :], ps_t[0:96, 0:P // 2].bitcast(BF16)).then_inc(tr_free, 1)

            def normalise(u, c):
                n = tr_at[("y", u, c)]
                dve.wait_ge(tr_ready, n + 1)
                part = ps_t[:, :].rearrange("p (t h w) -> p t h w", t=4, h=UH)
                if 2 * u + c:
                    dve.wait_ge(tr_free, n)
                chain(rec_ready, dve.reciprocal(rec[:, :, :], part[:, :, :, HD]))
                g = u % G
                if g == 0 and c == 0 and u:
                    dve.wait_ge(yt_raw, TB // 2 * (u // G))
                dst = y[:, 4 * c:4 * c + 4, UH * HD * g:UH * HD * (g + 1)].rearrange("p t (h w) -> p t h w", h=UH)
                dve.tensor_tensor(dst, part[:, :, :, 0:HD], rec[:, :, :].unsqueeze(3).to_broadcast([P, 4, UH, HD]),
                                  ALU.mult).then_inc(tr_free, 1)

            def add_projection(b):
                for i in range(TB):
                    dve.wait_ge(proj_raw, TB * b + i + 1)
                    t = TB * b + i
                    dve.tensor_tensor(x[:, t, :], ps_m[:, i % 2, 0:D], x[:, t, :], ALU.add).then_inc(proj_done, 1)

            def add_experts(t):
                dve.wait_ge(z_in[t % 2], 16 * (t // 2 + 1))
                dve.wait_ge(proj_done, t + 1)
                chain(sum_step, dve.scalar_tensor_tensor(x[:, t, :], z[:, t % 2, 0, :], gate[:, t, 0:1], x[:, t, :],
                                                         ALU.mult, ALU.add))
                dve.scalar_tensor_tensor(x[:, t, :], z[:, t % 2, 1, :], gate[:, t, 1:2], x[:, t, :],
                                         ALU.mult, ALU.add).then_inc(out_ready, 1)

            for k in range(QKS // 2):
                qk_parts(k)
                if k:
                    qk_lo_part(k - 1)
            qk_lo_part(QKS // 2 - 1)
            dve.wait_ge(consts, CONSTS)
            for t in range(NT):
                dve.wait_ge(v_raw, t + 1)
                dst = v[:, t, 0:H * VW].rearrange("p (h w) -> p h w", w=VW)[:, :, 0:HD]
                dve.tensor_tensor(dst, ps_m[:, t % 2, 0:H * HD].rearrange("p (h w) -> p h w", w=HD),
                                  bv[:, :].rearrange("p (h w) -> p h w", w=HD), ALU.add)
                dve.tensor_copy(lg[:, t, :], ps_m[:, t % 2, H * HD:H * HD + E]).then_inc(v_ready, 1)

            dve.wait_ge(v_ready, NT)
            for t in range(NT):
                ins = dve.max(top[:, t, :], lg[:, t, :])
            chain(route_step, ins)
            for t in range(NT):
                ins = dve.max_index(topi[:, t, :], top[:, t, :], lg[:, t, :])
            dve.tensor_tensor(dl[:, :], top[:, :, 1], top[:, :, 0], ALU.subtract).then_inc(gate_logit, 1)
            chain(route_step, ins)
            chain(route_step, dve.tensor_copy(topf[:, :, :], topi[:, :, 0:2]))
            for k in range(2):
                ins = dve.tensor_tensor(hot[:, k, :, :], iota8[:, :].unsqueeze(1).to_broadcast([P, NT, E]),
                                        topf[:, :, k:k + 1].to_broadcast([P, NT, E]), ALU.is_equal)
            chain(route_step, ins)
            dve.tensor_tensor(hots[:, :, :], hot[:, 0, :, :], hot[:, 1, :, :], ALU.add).then_inc(hots_ready, 1)

            def place_slots():
                dve.wait_ge(tr_ready, 1)
                chain(route_step, dve.tensor_tensor(fits[:, :, :], ps_t[:, P:P + E].unsqueeze(2).to_broadcast([P, E, NT]),
                                                    iota128[:, :].unsqueeze(1).to_broadcast([P, E, NT]), ALU.is_gt))
                chain(route_step, dve.tensor_reduce(ntile[:, :], fits[:, :, :], op=ALU.add, axis=AX.X))
                chain(route_step, dve.tensor_tensor_scan(tend[:, :], one8[:, :], ntile[:, :], 0.0, ALU.mult, ALU.add))
                chain(route_step, dve.tensor_tensor(sbase[:, :], tend[:, :], ntile[:, :], ALU.subtract))
                chain(route_step, dve.scalar_tensor_tensor(
                    place[:, :, :], sbase[:, :].unsqueeze(1).to_broadcast([P, NT, E]), float(P),
                    ps_t[:, 0:P].rearrange("p (t e) -> p t e", e=E), ALU.mult, ALU.add))
                for k in range(2):
                    ins = dve.tensor_tensor(prod[:, k, :, :], hot[:, k, :, :], place[:, :, :], ALU.mult)
                ins.then_inc(tr_free, 1)
                dve.wait_ge(tr_free, 1)
                chain(route_step, dve.tensor_reduce(posf[:, :, :], prod[:, :, :, :], op=ALU.add, axis=AX.X))
                chain(route_step, dve.tensor_copy(posi[:, :, :], posf[:, :, :]))
                dve.tensor_scalar(postile[:, :, :], posi[:, :, :], P.bit_length() - 1, None, ALU.logical_shift_right)
                chain(route_step, dve.tensor_scalar(posrow[:, :, :], posi[:, :, :], P - 1, None, ALU.bitwise_and))
                dve.scalar_tensor_tensor(pos[:, :, :], posrow[:, :, :], float(MAX_TILES), postile[:, :, :],
                                         ALU.mult, ALU.add).then_inc(pos_ready, 1)
                chain(route_step, dve.tensor_tensor(below[:, :, :], iota_t[:, :].unsqueeze(2).to_broadcast([P, MAX_TILES, E]),
                                                    tend[:, :].unsqueeze(1).to_broadcast([P, MAX_TILES, E]), ALU.is_ge))
                chain(route_step, dve.tensor_reduce(eidf[:, :], below[:, :, :], op=ALU.add, axis=AX.X))
                dve.tensor_scalar(eid[:, :], eidf[:, :], float(E - 1), None, ALU.min).then_inc(eid_ready, 1)
                dve.wait_ge(gate_exp, 1)
                chain(route_step, dve.tensor_scalar(dl[:, :], eg[:, :], 1.0, None, ALU.add))
                chain(route_step, dve.reciprocal(gate[:, :, 0], dl[:, :]))
                chain(route_step, dve.tensor_tensor(gate[:, :, 1], gate[:, :, 0], eg[:, :], ALU.mult))
                for t in range(NT):
                    ins = dve.tensor_tensor(x[:, t, :], x[:, t, :], bo[:, :], ALU.add)
                chain(route_step, ins)

            for k in range(QKS // 2, QKS):
                qk_parts(k)
                if k > QKS // 2:
                    qk_lo_part(k - 1)
                for m in range(6 * (k - QKS // 2), 6 * (k - QKS // 2) + 6):
                    row_max(0, m)
            qk_lo_part(QKS - 1)
            negate_max(0)
            place_slots()
            copy_neg(0)

            for u in range(UNITS):
                m = 0
                for n in range(NS):
                    if u + 1 < UNITS:
                        for m in range(CH_PER_STEP * n, min(CH_PER_STEP * (n + 1), NCH)):
                            row_max(u + 1, m)
                            if m == NCH - 1:
                                negate_max(u + 1)
                    if n == 5:
                        normalise(u, 0)
                    if n == 1 and u and u != G:
                        normalise(u - 1, 1)
                    if n == NS - 1 and u + 1 < UNITS:
                        copy_neg(u + 1)
                    if u == 2 and n == 5:
                        dve.wait_ge(list_in, 16)
                        chain(route_step, dve.tensor_scalar(clip[:, :], slots[:, :], float(2 * N - 1), None, ALU.min))
                        dve.tensor_scalar(token[:, :], clip[:, :], 1, None, ALU.logical_shift_right).then_inc(token_ready, 1)
                    if u >= G and n in (6, 10):
                        add_experts(2 * (u - G) + (n == 10))
                if u % G == G - 1:
                    normalise(u, 1)
                    add_projection(u // G)
                if u == G - 1:
                    for i in range(MAX_TILES):
                        dve.wait_ge(silu_ready, i + 1)
                        if i >= 2:
                            dve.wait_ge(hidt_raw, i - 1)
                        dve.scalar_tensor_tensor(hid[:, i % 2, :], silu[:, i % 2, :], LIMIT, ps_s[:, i % 2, F:2 * F],
                                                 ALU.min, ALU.mult).then_inc(hid_ready, 1)
                        dve.wait_ge(hidt_raw, i + 1)
                        if i >= 2:
                            dve.wait_ge(yo_raw, i - 1)
                        dve.tensor_copy(hidt[:, i % 2, :, :], ps_s[:, 3, 0:F].rearrange("p (c t) -> p c t", c=DC))\
                           .then_inc(hidt_ready, 1)
                        dve.wait_ge(yo_raw, i + 1)
                        if i >= 2:
                            dve.wait_ge(scatter_out[i % 2], 16 * (i // 2))
                        dve.tensor_copy(yo[:, i % 2, :], ps_m[:, i % 2, 0:D]).then_inc(yo_ready, 1)
            for t in range(TB, NT):
                add_experts(t)

        @block.tensor
        def _(pe):
            def transpose_xn(q):
                for c in range(DC):
                    r = DC * q + c
                    if r >= 4 and r < 8:
                        pe.wait_ge(qk_resid, QKS // 2)
                    for t in range(4):
                        if c == 0:
                            pe.wait_ge(xn_ready, 4 * q + t + 1)
                        ins = pe.transpose(ps_s[:, r % 4, P * t:P * (t + 1)], xn[:, 4 * q + t, P * c:P * (c + 1)],
                                           ident[:, :])
                    ins.then_inc(xnt_raw, 1)

            def project_qk(k):
                b, r = divmod(k, QKS // 2)
                op, r = divmod(r, 4)
                grp, n = divmod(r, 2)
                if k == 0:
                    pe.wait_ge(w_in, 16 * 6)
                    pe.wait_ge(xnt_ready, 4)
                if k == QKS // 2:
                    pe.wait_ge(xnt_ready, 8)
                if k % (QKS // 2) >= 4:
                    pe.wait_ge(qk_resid, k - 3)
                cols = slice(T * b + BANK * n, T * b + BANK * (n + 1))
                for c in range(DC):
                    ins = pe.matmul(ps_s[:, k % 4, :], wqk[:, op, c, P * grp:P * (grp + 1)], xnt_moe[:, c, cols],
                                    start=c == 0, stop=c == DC - 1)
                ins.then_inc(qk_raw, 1)

            def project_v(t):
                if t >= 2:
                    pe.wait_ge(v_ready, t - 1)
                for c in range(DC):
                    ins = pe.matmul(ps_m[:, t % 2, 0:H * HD + E], xnt_moe[:, c, P * t:P * (t + 1)], wvr[:, c, :],
                                    start=c == 0, stop=c == DC - 1)
                ins.then_inc(v_raw, 1)

            def route():
                pe.wait_ge(hots_ready, 1)
                pe.matmul(ps_t[:, 0:P], lower[:, :], hots[:, :, :], start=True, stop=False, skip_group_check=True)
                for t in range(NT - 1):
                    left = NT - 1 - t
                    pe.matmul(ps_t[:, E * (t + 1):P].rearrange("p (t e) -> p t e", e=E), ones[:, :],
                              hots[:, t:t + 1, :].to_broadcast([P, left, E]), start=False, stop=t == NT - 2,
                              skip_group_check=True)
                for t in range(NT):
                    ins = pe.matmul(ps_t[:, P:P + E], ones[:, :], hots[:, t, :], start=False, stop=t == NT - 1,
                                    skip_group_check=True)
                ins.then_inc(tr_ready, 1)

            def natural(u, m):
                h, i, s = CHUNKS[m]
                n = NCH * u + m
                width = min(P * (i + 1) - BANK * s, BANK)
                if m == 0:
                    pe.wait_ge(pack_in[u % SLOTS], 16 * PACKS * (u // SLOTS + 1))
                    if u >= SLOTS:
                        pe.wait_ge(maxrow_zero, u - SLOTS + 1)
                    if u == G + 1:
                        pe.wait_ge(yo_ready, MAX_TILES)
                if n < 2:
                    pe.wait_ge(v_ready, NT)
                else:
                    pe.wait_ge(max_done, n - 1)
                pe.matmul(ps_m[:, n % 2, 0:width], packq[0:KROWS, u % SLOTS, h, P * i:P * (i + 1)],
                          packk[0:KROWS, u % SLOTS, h, BANK * s:BANK * s + width], start=True, stop=True)\
                  .then_inc(nat_ready, 1)

            def transpose_neg(u):
                pe.wait_ge(neg_cols, u + 1)
                pe.wait_ge(tr_free, tr_at[("neg", u)])
                if u == G:
                    pass
                pe.transpose(ps_t[0:96, 0:P // 2].bitcast(BF16), negm[:, :, :, :].rearrange("p a h i -> p (a h i)"),
                             identb[:, :]).then_inc(tr_ready, 1)

            def scores(g):
                u, n = divmod(g, NS)
                t0, width = step_span(n)
                j = STEPS[n][1]
                if n == 0:
                    pe.wait_ge(neg_in[u % SLOTS], 16 * PARTS * (u // SLOTS + 1))
                for pr in range(2):
                    if g == 0:
                        pe.wait_ge(qk_resid, QKS)
                    elif g == NS * G:
                        pe.wait_ge(hidt_ready, MAX_TILES)
                        pe.wait_ge(probs_ready, 2 * (g - 1) + pr + 1)
                    else:
                        pe.wait_ge(probs_ready, 2 * (g - 1) + pr + 1)
                    for h in (2 * pr, 2 * pr + 1):
                        ins = pe.matmul(ps_s[:, h, 0:width], packk[0:KROWS, u % SLOTS, h, P * j:P * (j + 1)],
                                        packq[0:KROWS, u % SLOTS, h, t0:t0 + width], start=True, stop=True)
                    ins.then_inc(scores_ready, 1)

            def weigh_v(g):
                u, n = divmod(g, NS)
                c, j = STEPS[n]
                t0, width = step_span(n)
                b, gr = divmod(u, G)
                pe.wait_ge(probs_ready, 2 * g + 2)
                if diagonal(n):
                    pe.wait_ge(probs_masked, DIAG[NS] * u + DIAG[n + 1])
                if j == 0 and 2 * u + c:
                    pe.wait_ge(y_raw, 2 * u + c)
                last = (c + 1) * BANK // P - 1
                for h in range(UH):
                    at = VW * (UH * gr + h)
                    ins = pe.matmul(ps_y[32 * h:32 * h + 32, t0 - BANK * c:BANK], v[:, TB * b + j, at:at + 32],
                                    probs[:, g % 2, h, 0:width], start=j == 0, stop=j == last, skip_group_check=True)
                ins.then_inc(pv_done, 1)

            def transpose_y(u, c):
                pe.wait_ge(y_raw, 2 * u + c + 1)
                pe.wait_ge(tr_free, tr_at[("y", u, c)])
                if u == G:
                    pe.wait_ge(yt_ready, TB // 2)
                for t in range(4):
                    ins = pe.transpose(ps_t[:, P * t:P * (t + 1)], yraw[:, P * t:P * (t + 1)], ident[:, :])
                ins.then_inc(tr_ready, 1)

            def project(b):
                pe.wait_ge(tr_free, tr_at[("y", G * b + G - 1, 1)] + 1)
                for w in range(TB // 2):
                    if w:
                        pe.wait_ge(yt_ready, TB // 2 * b + w)
                    for a in range(2):
                        for c in range(DC):
                            ins = pe.transpose(ps_t[:, P * (2 * a + c):P * (2 * a + c + 1)],
                                               y[:, 2 * w + a, P * c:P * (c + 1)], ident[:, :])
                    ins.then_inc(yt_raw, 1)
                    pe.wait_ge(yt_ready, TB // 2 * b + w + 1)
                    for a in range(2):
                        i = 2 * w + a
                        if i >= 2:
                            pe.wait_ge(proj_done, TB * b + i - 1)
                        else:
                            pe.wait_ge(max_done, NCH * min(G * b + G + 1, UNITS))
                        for c in range(DC):
                            ins = pe.matmul(ps_m[:, i % 2, 0:D], yt[:, 2 * a + c, :], wo[:, c, :],
                                            start=c == 0, stop=c == DC - 1)
                        ins.then_inc(proj_raw, 1)

            def expert_in(i, slot, expert):
                if not isinstance(i, int) or i >= 1:
                    pe.wait_ge(xgt_ready, i)
                for c in range(DC):
                    ins = pe.transpose(ps_s[:, 2, P * c:P * (c + 1)], xg[:, slot, P * c:P * (c + 1)], ident[:, :])
                ins.then_inc(xgt_raw, 1)
                pe.wait_ge(xgt_ready, i + 1)
                if not isinstance(i, int) or i >= 2:
                    pe.wait_ge(hid_ready, i - 1)
                for c in range(DC):
                    ins = pe.matmul(ps_s[:, slot, :], xgt[:, slot, c, :],
                                    wgu[:, bass.ds(expert * (DC * 2 * F) + c * 2 * F, 2 * F)], start=c == 0, stop=c == DC - 1)
                ins.then_inc(gu_raw, 1)

            def expert_out(i, slot, expert):
                if not isinstance(i, int) or i >= 1:
                    pe.wait_ge(hidt_ready, i)
                pe.wait_ge(hid_ready, i + 1)
                for c in range(DC):
                    ins = pe.transpose(ps_s[:, 3, P * c:P * (c + 1)], hid[:, slot, P * c:P * (c + 1)], ident[:, :])
                ins.then_inc(hidt_raw, 1)
                pe.wait_ge(hidt_ready, i + 1)
                if not isinstance(i, int) or i >= 2:
                    pe.wait_ge(yo_ready, i - 1)
                for c in range(DC):
                    ins = pe.matmul(ps_m[:, slot, 0:D], hidt[:, slot, c, :],
                                    wd[:, bass.ds(expert * (DC * D) + c * D, D)], start=c == 0, stop=c == DC - 1)
                ins.then_inc(yo_raw, 1)

            def experts():
                pe.wait_ge(eid_ready, 1)
                pe.wait_ge(wgu_in, 16)
                pe.wait_ge(wd_in, 16)
                pe.wait_ge(proj_done, TB)
                pe.wait_ge(probs_ready, 2 * NS * G)

                def expert_of(i):
                    return pe.value_load(eid[0:1, i:i + 1], min_val=0, max_val=E - 1)

                before = expert_of(0)
                for i in range(MAX_TILES + 1):
                    if i < MAX_TILES:
                        now = expert_of(i) if i else before
                        pe.wait_ge(gather_in[i % 2], 16 * (i // 2 + 1))
                        expert_in(i, i % 2, now)
                    if i:
                        expert_out(i - 1, (i - 1) % 2, before)
                    before = now

            pe.wait_ge(consts, 2)
            transpose_xn(0)
            transpose_xn(1)
            for k in range(QKS // 2):
                project_qk(k)
            transpose_xn(2)
            transpose_xn(3)
            pe.wait_ge(xnt_ready, 8)
            for t in range(NT):
                project_v(t)
            for k in range(QKS // 2, QKS):
                project_qk(k)
                for m in range(6 * (k - QKS // 2), 6 * (k - QKS // 2) + 6):
                    if m == 0:
                        pe.wait_ge(consts, CONSTS)
                    natural(0, m)
                if k == QKS // 2:
                    route()
            transpose_neg(0)
            for u in range(UNITS):
                for n in range(NS):
                    g = NS * u + n
                    scores(g)
                    if u + 1 < UNITS:
                        for m in range(CH_PER_STEP * n, min(CH_PER_STEP * (n + 1), NCH)):
                            natural(u + 1, m)
                    if n or u % G:
                        weigh_v(g - 1)
                    if n == 5:
                        transpose_y(u, 0)
                    if n == 1 and u % G:
                        transpose_y(u - 1, 1)
                    if n == NS - 2 and u + 1 < UNITS:
                        transpose_neg(u + 1)
                if u % G == G - 1:
                    weigh_v(NS * (u + 1) - 1)
                    transpose_y(u, 1)
                    project(u // G)
                if u == G - 1:
                    experts()


_SHAPES = {
    "x": (N, D), "wqk": (P, 2, DC, H * HD), "wvr": (P, DC, H * HD + E), "bqk": (P, 2, 2), "bv": (H * HD,),
    "wo": (P, DC, D), "bo": (D,), "wgu": (P, E * DC * 2 * F), "wd": (P, E * DC * D),
}


def kernel(**inputs):
    import concourse.bacc as bacc
    from concourse.bass_utils import run_bass_kernel_spmd

    a = {k: np.asarray(val) for k, val in inputs.items()}

    def chunked(w):
        return w.reshape(-1, P, w.shape[-1]).transpose(1, 0, 2)

    def heads(w):
        return w.transpose(1, 0, 2).reshape(D, H * HD)

    def experts(w):
        return np.stack([chunked(m) for m in w], axis=1).reshape(P, -1)

    arrays = {
        "x": a["L0_attn_x"].reshape(N, D),
        "wqk": np.stack([chunked(heads(a["L0_attn_Wq"])), chunked(heads(a["L0_attn_Wk"]))], axis=1),
        "wvr": chunked(np.concatenate([heads(a["L0_attn_Wv"]), a["L0_ffn_Wr"]], axis=1)),
        "bqk": np.stack([a["L0_attn_bq"].reshape(2, P).T, a["L0_attn_bk"].reshape(2, P).T], axis=1),
        "bv": a["L0_attn_bv"].reshape(H * HD),
        "wo": chunked(a["L0_attn_Wo"]),
        "bo": a["L0_attn_bo"],
        "wgu": experts(np.concatenate([a["L0_ffn_Wg"], a["L0_ffn_Wu"]], axis=2)),
        "wd": experts(a["L0_ffn_Wd"]),
    }
    arrays = {f"in_{k}": np.ascontiguousarray(val) for k, val in arrays.items()}
    nc = bacc.Bacc("TRN2", target_bir_lowering=False, num_devices=1)
    args = {k: nc.dram_tensor(f"in_{k}", _SHAPES[k], F32, kind="ExternalInput").ap() for k in _SHAPES}
    out = nc.dram_tensor("out", (N, D), F32, kind="ExternalOutput").ap()
    build(nc, args["x"], args["wqk"], args["wvr"], args["bqk"], args["bv"], args["wo"], args["bo"], args["wgu"],
          args["wd"], out)
    r = run_bass_kernel_spmd(nc, [arrays], core_ids=[0])
    return r.results[0]["out"].reshape(B, T, D)
```

```python
from contextlib import ExitStack

import concourse.bass as bass
import numpy as np
from concourse import mybir

F32 = mybir.dt.float32
BF16 = mybir.dt.bfloat16
I32 = mybir.dt.int32
U32 = mybir.dt.uint32
ALU = mybir.AluOpType
ACT = mybir.ActivationFunctionType
AX = mybir.AxisListType

P = 128
B, T, D = 2, 1024, 256
H, HD = 16, 16
E, F = 8, 256
N = B * T
NT = N // P
TB = T // P
DC = D // P
EPS = 1e-5
SCALE = HD ** -0.5
LIMIT = 7.0
NEG = -3.0e38
BANK = 512

UH = 4
G = H // UH
UNITS = B * G
PARTS = 3
Q_PARTS = (0, 1, 2, 0, 1, 0)
K_PARTS = (0, 0, 0, 1, 1, 2)
MAXROW = HD * len(Q_PARTS)
KROWS = MAXROW + PARTS
SLOTS = 3
VW = HD + 1
VROW = H * VW + 32 - VW
STEPS = [(c, j) for c in range(T // BANK) for j in range((c + 1) * BANK // P)]
NS = len(STEPS)
CHUNKS = [(h, i, s) for h in range(UH) for i in range(TB) for s in range(i * P // BANK + 1)]
NCH = len(CHUNKS)
CH_PER_STEP = 5
QKS = B * 2 * (H * HD // P) * (T // BANK)

MAX_TILES = 2 * N // P + E - 1
PAD = 4 * N
CONSTS = 6
EXPERTS_FROM, EXPERTS_TO = 21, 74


def step_span(n):
    c, j = STEPS[n]
    t0 = max(P * j, BANK * c)
    return t0, BANK * (c + 1) - t0


def diagonal(n):
    c, j = STEPS[n]
    return P * j >= BANK * c


DIAG = [sum(diagonal(m) for m in range(n)) for n in range(NS + 1)]


def qk_tile(k):
    return k // 8, k // 4 % 2, k // 2 % 2, k % 2


def make_plan():
    plan = [("ln", 0), ("ln", 1)] + [("xnt", q, c) for q in range(2) for c in range(DC)]
    for k in range(4):
        plan += [("qk", k), ("qk_lo", k)]
    plan += [("store", 0), ("store", 1), ("load", 0), ("ln", 2), ("ln", 3)]
    fill = [[("qk", 4), ("qk_lo", 4)], [("v", 0)], [("v", 1)], [("qk", 5), ("qk_lo", 5), ("store", 2)], [("v", 2)], [("v", 3)],
            [("qk", 6), ("qk_lo", 6)], [("v", 4)], [("v", 5)], [("qk", 7), ("qk_lo", 7), ("store", 3), ("load", 1)],
            [("v", 6)], [("v", 7)], [("xnt", 2, 0)], [("xnt", 2, 1)], [("xnt", 3, 0)], [("xnt", 3, 1)]]
    fill += [[("v", t)] for t in range(TB, NT)] + [[("top",)]]
    m = 0
    for f, items in enumerate(fill):
        plan += items
        upto = max(0, (f - 5)) * NCH // (len(fill) - 6)
        plan += [("nat", 0, i) for i in range(m, upto)]
        m = max(m, upto)
    plan += [("negate", 0), ("load", 2), ("neg", 0), ("route",), ("place",)]

    beside = {g: [[], [], [], [], []] for g in range(NS * UNITS + 1)}
    for k in range(8):
        beside[k][0] += [("qk", 8 + k)]
        beside[k][1] += [("qk_lo", 8 + k)]
        if k % 2:
            beside[k][2] += [("store", 4 + k // 2)]
        beside[k][3] += [("wgu", k)]
        beside[k + 9][3] += [("wd", k)]
    for i in range(NT):
        beside[3 + i * 2 // 3][4] += [("list", i)]
    beside[14][4] += [("list_load",)]
    beside[17][4] += [("token",)]
    beside[18][4] += [("gather", 0), ("gather", 1)]
    project_at = [G * NS + 1 + t // 2 for t in range(TB)]
    free = [g for g in range(EXPERTS_FROM, EXPERTS_TO) if g not in project_at[2:]]
    steps = [free[i * len(free) // MAX_TILES] for i in range(MAX_TILES)]
    beside[steps[0] - 1][4] += [("moe_x", 0)]
    for i, g in enumerate(steps):
        beside[g][0] += [("moe_gu", i)]
        beside[g][1] += [("moe_hid", i)]
        beside[g][2] += [("moe_h", i)]
        if i + 1 < MAX_TILES:
            beside[g][3] += [("moe_x", i + 1)]
        if i + 2 < MAX_TILES:
            beside[g][4] += [("gather", i + 2)]
        beside[g][4] += [("moe_y", i), ("scatter", i)]
    for t, g in enumerate(project_at):
        q = (2 if t < 2 else 0) + t % 2
        beside[g][q] += [("proj_t", t)]
        beside[g][q + 1] += [("proj", t)]
    z_from = EXPERTS_TO + 2
    for t in range(NT):
        beside[z_from + t][1] += [("z_load", t)]
        beside[z_from + t + 3][2] += [("sum", t)]
        if t < TB:
            beside[z_from + t + 3][3] += [("out", t)]

    for g in range(NS * UNITS):
        u, n = divmod(g, NS)
        chunks = [("nat", u + 1, m) for m in range(CH_PER_STEP * n, min(CH_PER_STEP * (n + 1), NCH))]
        if u + 1 == UNITS:
            chunks = []
        half = (u, 0) if n == 5 else (u - 1, 1) if n == 1 and u else None
        for q in range(UH + 1):
            plan += [("s", g, q)] if q < UH else [("pv", g - 1)] if g else []
            plan += chunks[q:q + 1]
            if chunks[q:q + 1] and chunks[q][2] == NCH - 1:
                plan += [("negate", u + 1)]
            if q == 1 and half:
                plan += [("norm", *half)]
            plan += beside[g][q]
            if q == 0 and n == NS - 2 and u + 1 < UNITS:
                plan += [("neg", u + 1)]
            if q == 0 and n == 0 and u and u + 2 < UNITS:
                plan += [("load", u + 2)]
            if g and n in (4, 0) and q == UH:
                plan += [("y_copy", (g - 1) // NS, 0 if n == 4 else 1)]
            if q == 0 and half:
                plan += [("y_t", *half)]
    last = UNITS - 1
    plan += [("pv", NS * UNITS - 1), ("y_copy", last, 1), ("y_t", last, 1), ("norm", last, 1)]
    plan += [("proj_t", TB)]
    for t in range(TB, NT):
        plan += ([("proj_t", t + 1)] if t + 1 < NT else []) + [("proj", t), ("out", t)]
    return plan


PLAN = make_plan()


def bank_of(stage):
    kind = stage[0]
    if kind in ("xnt",):
        return stage[2] % 2
    if kind in ("qk", "v"):
        return stage[1] % 2
    if kind in ("route", "neg", "y_t", "moe_x", "moe_h", "moe_y", "proj_t"):
        return 0
    if kind in ("moe_gu", "proj"):
        return 1
    return None


FILLS = [[st for st in PLAN if bank_of(st) == bank] for bank in range(2)]
FILL_AT = {st: (bank, n) for bank in range(2) for n, st in enumerate(FILLS[bank])}


def build(nc, x_d, wqk_d, wvr_d, bqk_d, bv_d, wo_d, bo_d, wgu_d, wd_d, out_d):
    with ExitStack() as ctx:
        def sb(name, shape, dt=F32):
            return ctx.enter_context(nc.sbuf_tensor(name, shape, dt))

        def sem(name):
            return ctx.enter_context(nc.semaphore(name))

        xn_d = nc.dram_tensor("xn_rows", [N, D], F32).ap()
        qk_d = nc.dram_tensor("qk_parts", [2, PARTS, H, HD, N], BF16).ap()
        slot_d = nc.dram_tensor("slot_values", [MAX_TILES * P, 1], I32).ap()
        z_d = nc.dram_tensor("expert_rows", [2 * N, D], F32).ap()

        x = sb("x", [P, NT, D])
        xnt_moe = sb("xnt", [P, DC, N])
        wqk = sb("wqk", [P, 2, DC, H * HD])
        wvr = sb("wvr", [P, DC, H * HD + E])
        wo = sb("wo", [P, DC, D])
        bqk = sb("bqk", [P, 2, 2])
        bv = sb("bv", [P, H * HD])
        bo = sb("bo", [P, D])
        stats = sb("stats", [P, NT, 6])
        mv = sb("mv", [P, NT, 2])
        vareps = sb("vareps", [P, NT])
        rstd = sb("rstd", [P, NT])
        neghalf = sb("neghalf", [P, 4])
        stage = sb("stage", [P, 2, PARTS, T], BF16)
        resid = sb("resid", [P, 2, BANK])
        v = sb("v", [P, NT, VROW])
        packq = sb("packq", [P, SLOTS, UH, T], BF16)
        packk = sb("packk", [P, SLOTS, UH, T], BF16)
        probs = sb("probs", [P, 2, UH, BANK])
        xn = probs[:, :, :, :].rearrange("p a h n -> p (a h n)").rearrange("p (t d) -> p t d", d=D)
        maskrow = sb("maskrow", [P, BANK], BF16)
        mxa = sb("mxa", [P, 2, UH, TB])
        mxb = sb("mxb", [P, 2, UH, TB // 2])
        negm = sb("negm", [P, PARTS, UH, TB], BF16)
        negr = sb("negr", [P, UH, TB])
        negt = sb("negt", [P, P], BF16)
        yraw = sb("yraw", [P, BANK])
        rec = sb("rec", [P, 4, UH])
        y = sb("y", [P, TB, D])
        yt = sb("yt", [P, 2, DC, P])
        ident = sb("ident", [P, P])
        identb = sb("identb", [P, P], BF16)
        lower = sb("lower", [P, P], BF16)
        ones = sb("ones", [P, P], BF16)
        iota8 = sb("iota8", [P, E])
        iota128 = sb("iota128", [P, NT])
        iota_t = sb("iota_t", [P, MAX_TILES])
        slot_val = sb("slot_val", [P, NT, 2], I32)
        padv = sb("padv", [P, MAX_TILES], I32)
        lg = sb("lg", [P, NT, E])
        top = sb("top", [P, NT, E])
        topi = sb("topi", [P, NT, E], U32)
        topf = sb("topf", [P, NT, 2])
        dl = sb("dl", [P, NT])
        eg = sb("eg", [P, NT])
        gate = sb("gate", [P, NT, 2])
        hot = sb("hot", [P, 2, NT, E], BF16)
        hots = sb("hots", [P, NT, E], BF16)
        fits = sb("fits", [P, E, NT])
        ntile = sb("ntile", [P, E])
        tend = sb("tend", [P, E])
        one8 = sb("one8", [P, E])
        sbase = sb("sbase", [P, E])
        place = sb("place", [P, NT, E])
        prod = sb("prod", [P, 2, NT, E])
        posf = sb("posf", [P, 2, NT])
        posi = sb("posi", [P, 2, NT], I32)
        postile = sb("postile", [P, 2, NT], I32)
        posrow = sb("posrow", [P, 2, NT], I32)
        pos = sb("pos", [P, 2, NT], U32)
        below = sb("below", [P, MAX_TILES, E])
        eidf = sb("eidf", [P, MAX_TILES])
        eid = sb("eid", [P, MAX_TILES], I32)
        slots = sb("slots", [P, MAX_TILES], I32)
        clip = sb("clip", [P, MAX_TILES], I32)
        token = sb("token", [P, MAX_TILES], I32)
        wgu = sb("wgu", [P, E * DC * 2 * F])
        wd = xnt_moe[:, :, :].rearrange("p c n -> p (c n)")
        xg = sb("xg", [P, 2, D])
        xgt = sb("xgt", [P, 2, DC, P])
        silu = sb("silu", [P, 2, F])
        hid = sb("hid", [P, 2, F])
        hidt = sb("hidt", [P, 2, DC, P])
        yo = sb("yo", [P, 2, D])
        z = stage[:, :, :, :].rearrange("p a b t -> p (a b t)").bitcast(F32)[:, 0:2 * 2 * 2 * D // 2]
        z = z.rearrange("p (r k d) -> p r k d", r=2, k=2)

        ps_s = ctx.enter_context(nc.psum_tensor("ps_s", [P, 3, BANK], F32))
        ps_m = ctx.enter_context(nc.psum_tensor("ps_m", [P, 2, BANK], F32))
        ps_y = ctx.enter_context(nc.psum_tensor("ps_y", [P, BANK], F32))
        ps_w = ctx.enter_context(nc.psum_tensor("ps_w", [P, 2, BANK], F32))

        filled = [sem(f"filled{i}") for i in range(2)]
        freed = [sem(f"freed{i}") for i in range(2)]
        x_in = [sem(f"x_in{q}") for q in range(4)]
        wqk_in = sem("wqk_in")
        wvr_in = sem("wvr_in")
        wo_in = sem("wo_in")
        wgu_in = sem("wgu_in")
        wd_in = sem("wd_in")
        consts = sem("consts")
        const_step = sem("const_step")
        ln_step = sem("ln_step")
        var_ready = sem("var_ready")
        rstd_ready = sem("rstd_ready")
        xn_ready = sem("xn_ready")
        xn_out = sem("xn_out")
        xnt_ready = sem("xnt_ready")
        qk_hi = sem("qk_hi")
        qk_mid = sem("qk_mid")
        qk_lo = sem("qk_lo")
        qk_out = [sem(f"qk_out{i}") for i in range(2)]
        v_ready = sem("v_ready")
        pack_in = [sem(f"pack_in{i}") for i in range(SLOTS)]
        maxrow_zero = sem("maxrow_zero")
        nat_ready = sem("nat_ready")
        max_done = sem("max_done")
        neg_step = sem("neg_step")
        neg_cols = sem("neg_cols")
        neg_in = [sem(f"neg_in{i}") for i in range(SLOTS)]
        scores_ready = sem("scores_ready")
        probs_ready = sem("probs_ready")
        probs_masked = sem("probs_masked")
        pv_done = sem("pv_done")
        y_raw = sem("y_raw")
        rec_ready = sem("rec_ready")
        sum_step = sem("sum_step")
        route_step = sem("route_step")
        gate_logit = sem("gate_logit")
        gate_exp = sem("gate_exp")
        hots_ready = sem("hots_ready")
        pos_ready = sem("pos_ready")
        list_init = sem("list_init")
        list_out = sem("list_out")
        list_in = sem("list_in")
        eid_ready = sem("eid_ready")
        token_ready = sem("token_ready")
        gather_in = [sem(f"gather_in{i}") for i in range(2)]
        silu_ready = sem("silu_ready")
        scatter_out = [sem(f"scatter_out{i}") for i in range(2)]
        z_in = [sem(f"z_in{i}") for i in range(2)]
        summed = sem("summed")
        out_done = sem("out_done")

        def wait_room(pe, stage):
            bank, n = FILL_AT[stage]
            if n:
                pe.wait_ge(freed[bank], n)
            return bank, filled[bank]

        def wait_filled(eng, stage):
            bank, n = FILL_AT[stage]
            eng.wait_ge(filled[bank], n + 1)
            return bank

        def wait_freed(eng, stage):
            bank, n = FILL_AT[stage]
            eng.wait_ge(freed[bank], n + 1)

        def walk(stages):
            for kind, *args in PLAN:
                if kind in stages:
                    stages[kind](*args)

        PACKS = 2 * len(Q_PARTS)

        def span_rows(q):
            return slice(4 * q, 4 * q + 4)

        block = ctx.enter_context(nc.Block())

        @block.sync
        def _(sp):
            def store(w):
                b, grp, op, _ = qk_tile(2 * w)
                sp.wait_ge(qk_hi, 2 * w + 2)
                sp.wait_ge(qk_mid, 2 * w + 2)
                sp.wait_ge(qk_lo, 2 * w + 2)
                for part in range(PARTS):
                    dst = qk_d[op, part, 8 * grp:8 * grp + 8, :, T * b:T * b + T].rearrange("h d t -> (h d) t")
                    sp.dma_start(dst, stage[:, w % 2, part, :]).then_inc(qk_out[w % 2], 16)

            def load(u):
                b, g = divmod(u, G)
                heads, cols = slice(UH * g, UH * g + UH), slice(T * b, T * b + T)
                if u >= SLOTS:
                    sp.wait_ge(scores_ready, UH * NS * (u - SLOTS + 1))
                for s in qk_out:
                    sp.wait_ge(s, 16 * PARTS * (2 * b + g // 2 + 1))
                for op, (pack, parts) in enumerate(((packq, Q_PARTS), (packk, K_PARTS))):
                    for r, part in enumerate(parts):
                        sp.dma_start(pack[HD * r:HD * r + HD, u % SLOTS, :, :],
                                     qk_d[op, part, heads, :, cols].rearrange("h d t -> d h t"))\
                          .then_inc(pack_in[u % SLOTS], 16)

            def neg_rows(u):
                wait_freed(sp, ("neg", u))
                for part in range(PARTS):
                    dst = packq[MAXROW + part:MAXROW + part + 1, u % SLOTS, :, :]
                    sp.dma_start(dst.rearrange("o h (i t) -> o (h i) t", t=P),
                                 negt[32 * part:32 * part + 32, :]).then_inc(neg_in[u % SLOTS], 16)

            def load_wgu(e):
                w = E * DC * 2 * F // 8
                sp.dma_start(wgu[:, w * e:w * (e + 1)], wgu_d[:, w * e:w * (e + 1)]).then_inc(wgu_in, 16)

            def load_wd(e):
                w = E * DC * D // 8
                if e == 0:
                    for k in range(QKS - 2, QKS):
                        wait_freed(sp, ("qk", k))
                    for t in range(NT - 2, NT):
                        wait_freed(sp, ("v", t))
                sp.dma_start(wd[:, w * e:w * (e + 1)], wd_d[:, w * e:w * (e + 1)]).then_inc(wd_in, 16)

            def load_list():
                sp.wait_ge(list_out, 16 * 2 * NT)
                sp.dma_start(slots[:, :], slot_d.rearrange("(p i) o -> p (i o)", p=P)).then_inc(list_in, 16)

            def load_z(t):
                if t == 0:
                    for s in range(2):
                        sp.wait_ge(scatter_out[s], 16 * len(range(s, MAX_TILES, 2)))
                    for s in qk_out:
                        sp.wait_ge(s, 16 * PARTS * QKS // 4)
                if t >= 2:
                    sp.wait_ge(summed, t - 1)
                sp.dma_start(z[:, t % 2, :, :],
                             z_d[2 * P * t:2 * P * (t + 1), :].rearrange("(p k) d -> p k d", k=2)).then_inc(z_in[t % 2], 16)

            def store_out(t):
                if t < TB:
                    sp.wait_ge(summed, t + 1)
                else:
                    wait_freed(sp, ("proj", t))
                sp.dma_start(out_d[P * t:P * (t + 1), :], x[:, t, :]).then_inc(out_done, 16)

            def store_xn(q):
                sp.wait_ge(xn_ready, 4 * (q + 1))
                sp.dma_start(xn_d[P * 4 * q:P * 4 * (q + 1), :].rearrange("(t p) d -> p t d", p=P),
                             xn[:, span_rows(q), :]).then_inc(xn_out, 16)

            for q in range(4):
                sp.dma_start(x[:, span_rows(q), :],
                             x_d[P * 4 * q:P * 4 * (q + 1), :].rearrange("(t p) d -> p t d", p=P)).then_inc(x_in[q], 16)
            sp.wait_ge(consts, 1)
            sp.dma_start(slot_d.rearrange("(p c) o -> p (c o)", p=P), padv[:, :]).then_inc(list_init, 16)
            walk({"ln": store_xn, "store": store, "load": load, "neg": neg_rows, "wgu": load_wgu, "wd": load_wd,
                  "list_load": load_list, "z_load": load_z, "out": store_out})
            sp.wait_ge(out_done, 16 * NT)

        @block.gpsimd
        def _(pool):
            steps = [0]

            def chain(ins):
                ins.then_inc(const_step, 1)
                steps[0] += 1
                pool.wait_ge(const_step, steps[0])

            def inverse_deviation(q):
                pool.wait_ge(var_ready, q + 1)
                pool.tensor_tensor(rstd[:, span_rows(q)], vareps[:, span_rows(q)], neghalf[:, :], ALU.pow)\
                    .then_inc(rstd_ready, 1)

            pool.memset(padv[:, :], PAD).then_inc(consts, 1)
            chain(pool.memset(neghalf[:, :], -0.5))
            chain(pool.memset(ident[:, :], 0.0))
            chain(pool.affine_select(out=ident[:, :], in_=ident[:, :], compare_op=ALU.not_equal, fill=1.0, base=0,
                                     pattern=[[-1, P]], channel_multiplier=1))
            pool.tensor_copy(identb[:, :], ident[:, :]).then_inc(consts, 1)
            inverse_deviation(0)
            chain(pool.memset(maskrow[:, :], 0.0))
            pool.affine_select(out=maskrow[:, BANK - P:], in_=maskrow[:, BANK - P:], compare_op=ALU.is_ge, fill=NEG,
                               base=0, pattern=[[-1, P]], channel_multiplier=1).then_inc(consts, 1)
            inverse_deviation(1)
            chain(pool.memset(lower[:, :], 0.0))
            pool.affine_select(out=lower[:, :], in_=lower[:, :], compare_op=ALU.is_ge, fill=1.0, base=0,
                               pattern=[[-1, P]], channel_multiplier=1).then_inc(consts, 1)
            inverse_deviation(2)
            pool.memset(one8[:, :], 1.0)
            pool.iota(iota8[:, :], pattern=[[1, E]], base=0, channel_multiplier=0, allow_small_or_imprecise_dtypes=True)
            pool.iota(iota128[:, :], pattern=[[P, NT]], base=0, channel_multiplier=0,
                      allow_small_or_imprecise_dtypes=True)
            inverse_deviation(3)
            pool.iota(iota_t[:, :], pattern=[[1, MAX_TILES]], base=0, channel_multiplier=0,
                      allow_small_or_imprecise_dtypes=True)
            pool.iota(slot_val[:, :, :], pattern=[[2 * P, NT], [1, 2]], base=0, channel_multiplier=2).then_inc(consts, 1)
            chain(pool.memset(v[:, :, :], 1.0))
            chain(pool.memset(packq[MAXROW:KROWS, :, :, :], 0.0))
            chain(pool.memset(packk[MAXROW:KROWS, :, :, :], 1.0))
            pool.memset(ones[:, :], 1.0).then_inc(consts, 1)

            def place_tokens(i):
                if i == 0:
                    pool.wait_ge(pos_ready, 1)
                    pool.wait_ge(list_init, 16)
                for k in range(2):
                    pool.indirect_dma_start(out=slot_d, out_offset=bass.IndirectOffsetOnAxis(ap=pos[:, k, i:i + 1], axis=0),
                                            in_=slot_val[:, i, k:k + 1], in_offset=None).then_inc(list_out, 16)

            def gather(i):
                if i == 0:
                    pool.wait_ge(token_ready, 1)
                    pool.wait_ge(xn_out, 16 * 4)
                if i >= 2:
                    wait_filled(pool, ("moe_x", i - 2))
                pool.indirect_dma_start(out=xg[:, i % 2, :], out_offset=None, in_=xn_d,
                                        in_offset=bass.IndirectOffsetOnAxis(ap=token[:, i:i + 1], axis=0))\
                    .then_inc(gather_in[i % 2], 16)

            def scatter(i):
                wait_freed(pool, ("moe_y", i))
                pool.indirect_dma_start(out=z_d, out_offset=bass.IndirectOffsetOnAxis(ap=slots[:, i:i + 1], axis=0),
                                        in_=yo[:, i % 2, :], in_offset=None, bounds_check=2 * N - 1, oob_is_err=False)\
                    .then_inc(scatter_out[i % 2], 16)

            def mask(g, h):
                u, n = divmod(g, NS)
                if h == UH - 1 and diagonal(n):
                    pool.wait_ge(probs_ready, UH * (g + 1))
                    cols = probs[:, g % 2, :, 0:P]
                    pool.affine_select(out=cols, in_=cols, compare_op=ALU.is_ge, fill=0.0, base=0,
                                       pattern=[[0, UH], [1, P]], channel_multiplier=-1).then_inc(probs_masked, 1)

            def zero_rows(u):
                if u >= SLOTS:
                    pool.wait_ge(scores_ready, UH * NS * (u - SLOTS + 1))
                    pool.wait_ge(probs_masked, DIAG[NS] * (u - 2))
                    pool.memset(packq[MAXROW:KROWS, u % SLOTS, :, :], 0.0).then_inc(maxrow_zero, 1)
                    pool.wait_ge(maxrow_zero, u - SLOTS + 1)

            walk({"list": place_tokens, "gather": gather, "scatter": scatter, "s": mask, "load": zero_rows})

        @block.scalar
        def _(act):
            def copy_xnt(q, c):
                bank = wait_filled(act, ("xnt", q, c))
                act.copy(xnt_moe[:, c, 4 * P * q:4 * P * (q + 1)], ps_w[:, bank, :]).then_inc(freed[bank], 1)

            def qk_hi_part(k):
                _, grp, op, n = qk_tile(k)
                w = k // 2
                if k == 0:
                    act.wait_ge(wqk_in, 32)
                bank = wait_filled(act, ("qk", k))
                if w >= 2:
                    act.wait_ge(qk_out[w % 2], 16 * PARTS * (w // 2))
                act.activation(stage[:, w % 2, 0, BANK * n:BANK * (n + 1)], ps_w[:, bank, :], ACT.Identity,
                               bias=bqk[:, op, grp:grp + 1], scale=1.0).then_inc(qk_hi, 1)

            def qk_mid_part(k):
                wait_freed(act, ("qk", k))
                act.copy(stage[:, k // 2 % 2, 1, BANK * (k % 2):BANK * (k % 2 + 1)], resid[:, k % 2, :]).then_inc(qk_mid, 1)

            def gates():
                act.wait_ge(gate_logit, 1)
                act.activation(eg[:, :], dl[:, :], ACT.Exp).then_inc(gate_exp, 1)

            def exps(g, h):
                _, width = step_span(g % NS)
                k = UH * g + h
                act.wait_ge(scores_ready, k + 1)
                if g == 0 and h == 0:
                    act.wait_ge(xn_out, 16 * 4)
                if g >= 2 and h == 0:
                    act.wait_ge(pv_done, g - 1)
                act.activation(probs[:, g % 2, h, 0:width], ps_s[:, k % 3, 0:width], ACT.Exp, scale=SCALE)\
                   .then_inc(probs_ready, 1)

            def copy_y(u, c):
                act.wait_ge(pv_done, NS * u + (4 if c == 0 else NS))
                if 2 * u + c:
                    wait_filled(act, ("y_t", *divmod(2 * u + c - 1, 2)))
                act.copy(yraw[:, :], ps_y[:, :]).then_inc(y_raw, 1)

            def copy_yt(t):
                bank = wait_filled(act, ("proj_t", t))
                if t >= 2:
                    wait_filled(act, ("proj", t - 2))
                act.copy(yt[:, t % 2, :, :], ps_w[:, bank, 0:D].rearrange("p (a t) -> p a t", a=DC)).then_inc(freed[bank], 1)

            def copy_xgt(i):
                bank = wait_filled(act, ("moe_x", i))
                if i >= 2:
                    wait_filled(act, ("moe_gu", i - 2))
                act.copy(xgt[:, i % 2, :, :], ps_w[:, bank, 0:D].rearrange("p (c t) -> p c t", c=DC)).then_inc(freed[bank], 1)

            def silu_gate(i):
                bank = wait_filled(act, ("moe_gu", i))
                if i >= 2:
                    wait_freed(act, ("moe_gu", i - 2))
                act.activation(silu[:, i % 2, :], ps_w[:, bank, 0:F], ACT.Silu).then_inc(silu_ready, 1)

            def copy_hidt(i):
                bank = wait_filled(act, ("moe_h", i))
                if i >= 2:
                    wait_filled(act, ("moe_y", i - 2))
                act.copy(hidt[:, i % 2, :, :], ps_w[:, bank, 0:F].rearrange("p (c t) -> p c t", c=DC)).then_inc(freed[bank], 1)

            def copy_yo(i):
                bank = wait_filled(act, ("moe_y", i))
                if i >= 2:
                    act.wait_ge(scatter_out[i % 2], 16 * (i // 2))
                act.copy(yo[:, i % 2, :], ps_w[:, bank, 0:D]).then_inc(freed[bank], 1)

            act.dma_start(wqk[:, :, :, :], wqk_d).then_inc(wqk_in, 16)
            act.dma_start(bqk[:, :, :], bqk_d).then_inc(wqk_in, 16)
            act.dma_start(wvr[:, :, :], wvr_d).then_inc(wvr_in, 16)
            act.dma_start(bv[:, :], bv_d.partition_broadcast(P)).then_inc(wvr_in, 16)
            act.dma_start(wo[:, :, :], wo_d).then_inc(wo_in, 16)
            act.dma_start(bo[:, :], bo_d.partition_broadcast(P)).then_inc(wo_in, 16)
            walk({"xnt": copy_xnt, "qk": qk_hi_part, "qk_lo": qk_mid_part, "top": gates, "s": exps, "y_copy": copy_y,
                  "proj_t": copy_yt, "moe_x": copy_xgt, "moe_gu": silu_gate, "moe_h": copy_hidt, "moe_y": copy_yo})

        @block.vector
        def _(dve):
            count = {}

            def chain(s, ins):
                ins.then_inc(s, 1)
                count[s.name] = count.get(s.name, 0) + 1
                dve.wait_ge(s, count[s.name])

            def layernorm(q):
                dve.wait_ge(x_in[q], 16)
                for t in range(4 * q, 4 * q + 4):
                    ins = dve.bn_stats(stats[:, t, :], x[:, t, :])
                chain(ln_step, ins)
                for t in range(4 * q, 4 * q + 4):
                    ins = dve.bn_aggr(mv[:, t, :], stats[:, t, :])
                chain(ln_step, ins)
                dve.tensor_scalar(vareps[:, span_rows(q)], mv[:, span_rows(q), 1], EPS, None, ALU.add).then_inc(var_ready, 1)
                dve.wait_ge(rstd_ready, q + 1)
                for t in range(4 * q, 4 * q + 4):
                    dve.tensor_scalar(xn[:, t, :], x[:, t, :], mv[:, t, 0:1], rstd[:, t:t + 1], ALU.subtract, ALU.mult)\
                       .then_inc(xn_ready, 1)

            def qk_resid_part(k):
                _, grp, op, n = qk_tile(k)
                bank, _ = FILL_AT[("qk", k)]
                dve.wait_ge(qk_hi, k + 1)
                if k >= 2:
                    dve.wait_ge(qk_lo, k - 1)
                dve.scalar_tensor_tensor(resid[:, k % 2, :], ps_w[:, bank, :], bqk[:, op, grp:grp + 1],
                                         stage[:, k // 2 % 2, 0, BANK * n:BANK * (n + 1)], ALU.add, ALU.subtract)\
                   .then_inc(freed[bank], 1)

            def qk_lo_part(k):
                w, n = divmod(k, 2)
                cols = slice(BANK * n, BANK * (n + 1))
                dve.wait_ge(qk_mid, k + 1)
                dve.tensor_tensor(stage[:, w % 2, 2, cols], resid[:, k % 2, :], stage[:, w % 2, 1, cols],
                                  ALU.subtract).then_inc(qk_lo, 1)

            def add_v_bias(t):
                if t == 0:
                    dve.wait_ge(wvr_in, 32)
                    dve.wait_ge(consts, CONSTS)
                bank = wait_filled(dve, ("v", t))
                dst = v[:, t, 0:H * VW].rearrange("p (h w) -> p h w", w=VW)[:, :, 0:HD]
                dve.tensor_tensor(dst, ps_w[:, bank, 0:H * HD].rearrange("p (h w) -> p h w", w=HD),
                                  bv[:, :].rearrange("p (h w) -> p h w", w=HD), ALU.add).then_inc(v_ready, 1)
                dve.tensor_copy(lg[:, t, :], ps_w[:, bank, H * HD:H * HD + E]).then_inc(freed[bank], 1)

            def row_max(u, m):
                h, i, s = CHUNKS[m]
                n = NCH * u + m
                width = min(P * (i + 1) - BANK * s, BANK)
                into = mxa[:, u % 2, h, i:i + 1] if s == 0 else mxb[:, u % 2, h, i - TB // 2:i - TB // 2 + 1]
                dve.wait_ge(nat_ready, n + 1)
                if s == i * P // BANK:
                    ins = dve.tensor_tensor_reduce(out=ps_m[:, n % 2, 0:width], in0=ps_m[:, n % 2, 0:width],
                                                   in1=maskrow[:, BANK - width:], scale=1.0, scalar=NEG,
                                                   op0=ALU.add, op1=ALU.max, accum_out=into)
                else:
                    ins = dve.tensor_reduce(into, ps_m[:, n % 2, 0:width], op=ALU.max, axis=AX.X)
                ins.then_inc(max_done, 1)

            def negate_max(u):
                dve.wait_ge(max_done, NCH * (u + 1))
                m = mxa[:, u % 2, :, :]
                chain(neg_step, dve.tensor_tensor(m[:, :, TB // 2:], m[:, :, TB // 2:], mxb[:, u % 2, :, :], ALU.max))
                if u:
                    wait_filled(dve, ("neg", u - 1))
                chain(neg_step, dve.tensor_scalar(negm[:, 0, :, :], m, -1.0, None, ALU.mult))
                chain(neg_step, dve.scalar_tensor_tensor(negr[:, :, :], m, -1.0, negm[:, 0, :, :], ALU.mult, ALU.subtract))
                chain(neg_step, dve.tensor_copy(negm[:, 1, :, :], negr[:, :, :]))
                dve.tensor_tensor(negm[:, 2, :, :], negr[:, :, :], negm[:, 1, :, :], ALU.subtract).then_inc(neg_cols, 1)

            def copy_neg(u):
                bank = wait_filled(dve, ("neg", u))
                if u:
                    dve.wait_ge(neg_in[(u - 1) % SLOTS], 16 * PARTS * ((u - 1) // SLOTS + 1))
                dve.tensor_copy(negt[0:96, :], ps_w[0:96, bank, 0:P // 2].bitcast(BF16)).then_inc(freed[bank], 1)

            def normalise(u, c):
                bank = wait_filled(dve, ("y_t", u, c))
                part = ps_w[:, bank, :].rearrange("p (t h w) -> p t h w", t=4, h=UH)
                chain(rec_ready, dve.reciprocal(rec[:, :, :], part[:, :, :, HD]))
                g = u % G
                if u == G and c == 0:
                    wait_filled(dve, ("proj_t", TB - 1))
                dst = y[:, 4 * c:4 * c + 4, UH * HD * g:UH * HD * (g + 1)].rearrange("p t (h w) -> p t h w", h=UH)
                dve.tensor_tensor(dst, part[:, :, :, 0:HD], rec[:, :, :].unsqueeze(3).to_broadcast([P, 4, UH, HD]),
                                  ALU.mult).then_inc(freed[bank], 1)

            def add_experts(t):
                dve.wait_ge(z_in[t % 2], 16 * (t // 2 + 1))
                if t < TB:
                    wait_freed(dve, ("proj", t))
                chain(sum_step, dve.scalar_tensor_tensor(x[:, t, :], z[:, t % 2, 0, :], gate[:, t, 0:1], x[:, t, :],
                                                         ALU.mult, ALU.add))
                dve.scalar_tensor_tensor(x[:, t, :], z[:, t % 2, 1, :], gate[:, t, 1:2], x[:, t, :],
                                         ALU.mult, ALU.add).then_inc(summed, 1)

            def add_projection(t):
                bank = wait_filled(dve, ("proj", t))
                if t >= TB:
                    dve.wait_ge(summed, t + 1)
                dve.tensor_tensor(x[:, t, :], ps_w[:, bank, 0:D], x[:, t, :], ALU.add).then_inc(freed[bank], 1)

            def best_two():
                for t in range(NT - 2, NT):
                    wait_freed(dve, ("v", t))
                dve.wait_ge(consts, CONSTS)
                for t in range(NT):
                    ins = dve.max(top[:, t, :], lg[:, t, :])
                chain(route_step, ins)
                for t in range(NT):
                    ins = dve.max_index(topi[:, t, :], top[:, t, :], lg[:, t, :])
                dve.tensor_tensor(dl[:, :], top[:, :, 1], top[:, :, 0], ALU.subtract).then_inc(gate_logit, 1)
                chain(route_step, ins)
                chain(route_step, dve.tensor_copy(topf[:, :, :], topi[:, :, 0:2]))
                for k in range(2):
                    ins = dve.tensor_tensor(hot[:, k, :, :], iota8[:, :].unsqueeze(1).to_broadcast([P, NT, E]),
                                            topf[:, :, k:k + 1].to_broadcast([P, NT, E]), ALU.is_equal)
                chain(route_step, ins)
                dve.tensor_tensor(hots[:, :, :], hot[:, 0, :, :], hot[:, 1, :, :], ALU.add).then_inc(hots_ready, 1)

            def place_slots():
                wait_filled(dve, ("route",))
                chain(route_step, dve.tensor_tensor(fits[:, :, :], ps_w[:, 0, P:P + E].unsqueeze(2).to_broadcast([P, E, NT]),
                                                    iota128[:, :].unsqueeze(1).to_broadcast([P, E, NT]), ALU.is_gt))
                chain(route_step, dve.tensor_reduce(ntile[:, :], fits[:, :, :], op=ALU.add, axis=AX.X))
                chain(route_step, dve.tensor_tensor_scan(tend[:, :], one8[:, :], ntile[:, :], 0.0, ALU.mult, ALU.add))
                chain(route_step, dve.tensor_tensor(sbase[:, :], tend[:, :], ntile[:, :], ALU.subtract))
                chain(route_step, dve.scalar_tensor_tensor(
                    place[:, :, :], sbase[:, :].unsqueeze(1).to_broadcast([P, NT, E]), float(P),
                    ps_w[:, 0, 0:P].rearrange("p (t e) -> p t e", e=E), ALU.mult, ALU.add))
                for k in range(2):
                    ins = dve.tensor_tensor(prod[:, k, :, :], hot[:, k, :, :], place[:, :, :], ALU.mult)
                ins.then_inc(freed[0], 1)
                wait_freed(dve, ("route",))
                chain(route_step, dve.tensor_reduce(posf[:, :, :], prod[:, :, :, :], op=ALU.add, axis=AX.X))
                chain(route_step, dve.tensor_copy(posi[:, :, :], posf[:, :, :]))
                dve.tensor_scalar(postile[:, :, :], posi[:, :, :], P.bit_length() - 1, None, ALU.logical_shift_right)
                chain(route_step, dve.tensor_scalar(posrow[:, :, :], posi[:, :, :], P - 1, None, ALU.bitwise_and))
                dve.scalar_tensor_tensor(pos[:, :, :], posrow[:, :, :], float(MAX_TILES), postile[:, :, :],
                                         ALU.mult, ALU.add).then_inc(pos_ready, 1)
                chain(route_step, dve.tensor_tensor(below[:, :, :], iota_t[:, :].unsqueeze(2).to_broadcast([P, MAX_TILES, E]),
                                                    tend[:, :].unsqueeze(1).to_broadcast([P, MAX_TILES, E]), ALU.is_ge))
                chain(route_step, dve.tensor_reduce(eidf[:, :], below[:, :, :], op=ALU.add, axis=AX.X))
                dve.tensor_scalar(eid[:, :], eidf[:, :], float(E - 1), None, ALU.min).then_inc(eid_ready, 1)
                dve.wait_ge(gate_exp, 1)
                chain(route_step, dve.tensor_scalar(dl[:, :], eg[:, :], 1.0, None, ALU.add))
                chain(route_step, dve.reciprocal(gate[:, :, 0], dl[:, :]))
                chain(route_step, dve.tensor_tensor(gate[:, :, 1], gate[:, :, 0], eg[:, :], ALU.mult))
                dve.wait_ge(wo_in, 32)
                for t in range(NT):
                    ins = dve.tensor_tensor(x[:, t, :], x[:, t, :], bo[:, :], ALU.add)
                chain(route_step, ins)

            def token_of_slot():
                dve.wait_ge(list_in, 16)
                chain(route_step, dve.tensor_scalar(clip[:, :], slots[:, :], float(2 * N - 1), None, ALU.min))
                dve.tensor_scalar(token[:, :], clip[:, :], 1, None, ALU.logical_shift_right).then_inc(token_ready, 1)

            def hidden(i):
                bank, _ = FILL_AT[("moe_gu", i)]
                dve.wait_ge(silu_ready, i + 1)
                if i >= 2:
                    wait_filled(dve, ("moe_h", i - 2))
                dve.scalar_tensor_tensor(hid[:, i % 2, :], silu[:, i % 2, :], LIMIT, ps_w[:, bank, F:2 * F],
                                         ALU.min, ALU.mult).then_inc(freed[bank], 1)

            walk({"ln": layernorm, "qk": qk_resid_part, "qk_lo": qk_lo_part, "v": add_v_bias, "nat": row_max,
                  "negate": negate_max, "neg": copy_neg, "norm": normalise, "sum": add_experts, "proj": add_projection,
                  "top": best_two, "place": place_slots, "token": token_of_slot, "moe_hid": hidden})

        @block.tensor
        def _(pe):
            expert = {}

            def transpose_xn(q, c):
                if q == 0 and c == 0:
                    pe.wait_ge(consts, 2)
                bank, full = wait_room(pe, ("xnt", q, c))
                pe.wait_ge(xn_ready, 4 * q + 4)
                for t in range(4):
                    ins = pe.transpose(ps_w[:, bank, P * t:P * (t + 1)], xn[:, 4 * q + t, P * c:P * (c + 1)], ident[:, :])
                ins.then_inc(full, 1)

            def project_qk(k):
                b, grp, op, n = qk_tile(k)
                if k % 8 == 0:
                    pe.wait_ge(wqk_in, 32)
                    for c in range(DC):
                        wait_freed(pe, ("xnt", 2 * b + 1, c))
                bank, full = wait_room(pe, ("qk", k))
                cols = slice(T * b + BANK * n, T * b + BANK * (n + 1))
                for c in range(DC):
                    ins = pe.matmul(ps_w[:, bank, :], wqk[:, op, c, P * grp:P * (grp + 1)], xnt_moe[:, c, cols],
                                    start=c == 0, stop=c == DC - 1)
                ins.then_inc(full, 1)

            def project_v(t):
                if t == 0:
                    pe.wait_ge(wvr_in, 32)
                if t == TB:
                    for c in range(DC):
                        wait_freed(pe, ("xnt", 3, c))
                bank, full = wait_room(pe, ("v", t))
                for c in range(DC):
                    ins = pe.matmul(ps_w[:, bank, 0:H * HD + E], xnt_moe[:, c, P * t:P * (t + 1)], wvr[:, c, :],
                                    start=c == 0, stop=c == DC - 1)
                ins.then_inc(full, 1)

            def route():
                pe.wait_ge(hots_ready, 1)
                bank, full = wait_room(pe, ("route",))
                pe.matmul(ps_w[:, bank, 0:P], lower[:, :], hots[:, :, :], start=True, stop=False, skip_group_check=True)
                for t in range(NT - 1):
                    left = NT - 1 - t
                    pe.matmul(ps_w[:, bank, E * (t + 1):P].rearrange("p (t e) -> p t e", e=E), ones[:, :],
                              hots[:, t:t + 1, :].to_broadcast([P, left, E]), start=False, stop=t == NT - 2,
                              skip_group_check=True)
                for t in range(NT):
                    ins = pe.matmul(ps_w[:, bank, P:P + E], ones[:, :], hots[:, t, :], start=False, stop=t == NT - 1,
                                    skip_group_check=True)
                ins.then_inc(full, 1)

            def natural(u, m):
                h, i, s = CHUNKS[m]
                n = NCH * u + m
                width = min(P * (i + 1) - BANK * s, BANK)
                if m == 0:
                    pe.wait_ge(consts, CONSTS)
                    pe.wait_ge(pack_in[u % SLOTS], 16 * PACKS * (u // SLOTS + 1))
                    if u >= SLOTS:
                        pe.wait_ge(maxrow_zero, u - SLOTS + 1)
                if n >= 2:
                    pe.wait_ge(max_done, n - 1)
                pe.matmul(ps_m[:, n % 2, 0:width], packq[0:KROWS, u % SLOTS, h, P * i:P * (i + 1)],
                          packk[0:KROWS, u % SLOTS, h, BANK * s:BANK * s + width], start=True, stop=True)\
                  .then_inc(nat_ready, 1)

            def transpose_neg(u):
                pe.wait_ge(neg_cols, u + 1)
                bank, full = wait_room(pe, ("neg", u))
                pe.transpose(ps_w[0:96, bank, 0:P // 2].bitcast(BF16), negm[:, :, :, :].rearrange("p a h i -> p (a h i)"),
                             identb[:, :]).then_inc(full, 1)

            def scores(g, h):
                u, n = divmod(g, NS)
                t0, width = step_span(n)
                j = STEPS[n][1]
                k = UH * g + h
                if n == 0 and h == 0:
                    pe.wait_ge(neg_in[u % SLOTS], 16 * PARTS * (u // SLOTS + 1))
                if k >= 3:
                    pe.wait_ge(probs_ready, k - 2)
                pe.matmul(ps_s[:, k % 3, 0:width], packk[0:KROWS, u % SLOTS, h, P * j:P * (j + 1)],
                          packq[0:KROWS, u % SLOTS, h, t0:t0 + width], start=True, stop=True).then_inc(scores_ready, 1)

            def weigh_v(g):
                u, n = divmod(g, NS)
                c, j = STEPS[n]
                t0, width = step_span(n)
                b, gr = divmod(u, G)
                if g == 0:
                    pe.wait_ge(v_ready, NT)
                pe.wait_ge(probs_ready, UH * (g + 1))
                if diagonal(n):
                    pe.wait_ge(probs_masked, DIAG[NS] * u + DIAG[n + 1])
                if j == 0 and 2 * u + c:
                    pe.wait_ge(y_raw, 2 * u + c)
                last = (c + 1) * BANK // P - 1
                for h in range(UH):
                    at = VW * (UH * gr + h)
                    ins = pe.matmul(ps_y[32 * h:32 * h + 32, t0 - BANK * c:BANK], v[:, TB * b + j, at:at + 32],
                                    probs[:, g % 2, h, 0:width], start=j == 0, stop=j == last, skip_group_check=True)
                ins.then_inc(pv_done, 1)

            def transpose_y(u, c):
                pe.wait_ge(y_raw, 2 * u + c + 1)
                bank, full = wait_room(pe, ("y_t", u, c))
                for t in range(4):
                    ins = pe.transpose(ps_w[:, bank, P * t:P * (t + 1)], yraw[:, P * t:P * (t + 1)], ident[:, :])
                ins.then_inc(full, 1)

            def transpose_heads(t):
                if t % TB == 0:
                    wait_freed(pe, ("y_t", G * (t // TB) + G - 1, 1))
                bank, full = wait_room(pe, ("proj_t", t))
                for c in range(DC):
                    ins = pe.transpose(ps_w[:, bank, P * c:P * (c + 1)], y[:, t % TB, P * c:P * (c + 1)], ident[:, :])
                ins.then_inc(full, 1)

            def project(t):
                if t == 0:
                    pe.wait_ge(wo_in, 32)
                wait_freed(pe, ("proj_t", t))
                bank, full = wait_room(pe, ("proj", t))
                for c in range(DC):
                    ins = pe.matmul(ps_w[:, bank, 0:D], yt[:, t % 2, c, :], wo[:, c, :], start=c == 0, stop=c == DC - 1)
                ins.then_inc(full, 1)

            def transpose_rows(i):
                pe.wait_ge(gather_in[i % 2], 16 * (i // 2 + 1))
                bank, full = wait_room(pe, ("moe_x", i))
                for c in range(DC):
                    ins = pe.transpose(ps_w[:, bank, P * c:P * (c + 1)], xg[:, i % 2, P * c:P * (c + 1)], ident[:, :])
                ins.then_inc(full, 1)

            def gate_up(i):
                if i == 0:
                    pe.wait_ge(eid_ready, 1)
                    pe.wait_ge(wgu_in, 16 * 8)
                    pe.wait_ge(wd_in, 16 * 8)
                expert[i] = pe.value_load(eid[0:1, i:i + 1], min_val=0, max_val=E - 1)
                wait_freed(pe, ("moe_x", i))
                bank, full = wait_room(pe, ("moe_gu", i))
                for c in range(DC):
                    ins = pe.matmul(ps_w[:, bank, :], xgt[:, i % 2, c, :],
                                    wgu[:, bass.ds(expert[i] * (DC * 2 * F) + c * 2 * F, 2 * F)],
                                    start=c == 0, stop=c == DC - 1)
                ins.then_inc(full, 1)

            def transpose_hidden(i):
                wait_freed(pe, ("moe_gu", i))
                bank, full = wait_room(pe, ("moe_h", i))
                for c in range(DC):
                    ins = pe.transpose(ps_w[:, bank, P * c:P * (c + 1)], hid[:, i % 2, P * c:P * (c + 1)], ident[:, :])
                ins.then_inc(full, 1)

            def down(i):
                wait_freed(pe, ("moe_h", i))
                bank, full = wait_room(pe, ("moe_y", i))
                for c in range(DC):
                    ins = pe.matmul(ps_w[:, bank, 0:D], hidt[:, i % 2, c, :],
                                    wd[:, bass.ds(expert[i] * (DC * D) + c * D, D)], start=c == 0, stop=c == DC - 1)
                ins.then_inc(full, 1)

            walk({"xnt": transpose_xn, "qk": project_qk, "v": project_v, "route": route, "nat": natural,
                  "neg": transpose_neg, "s": scores, "pv": weigh_v, "y_t": transpose_y, "proj_t": transpose_heads,
                  "proj": project, "moe_x": transpose_rows, "moe_gu": gate_up, "moe_h": transpose_hidden,
                  "moe_y": down})


_SHAPES = {
    "x": (N, D), "wqk": (P, 2, DC, H * HD), "wvr": (P, DC, H * HD + E), "bqk": (P, 2, 2), "bv": (H * HD,),
    "wo": (P, DC, D), "bo": (D,), "wgu": (P, E * DC * 2 * F), "wd": (P, E * DC * D),
}


def kernel(**inputs):
    import concourse.bacc as bacc
    from concourse.bass_utils import run_bass_kernel_spmd

    a = {k: np.asarray(val) for k, val in inputs.items()}

    def chunked(w):
        return w.reshape(-1, P, w.shape[-1]).transpose(1, 0, 2)

    def heads(w):
        return w.transpose(1, 0, 2).reshape(D, H * HD)

    def experts(w):
        return np.stack([chunked(m) for m in w], axis=1).reshape(P, -1)

    arrays = {
        "x": a["L0_attn_x"].reshape(N, D),
        "wqk": np.stack([chunked(heads(a["L0_attn_Wq"])), chunked(heads(a["L0_attn_Wk"]))], axis=1),
        "wvr": chunked(np.concatenate([heads(a["L0_attn_Wv"]), a["L0_ffn_Wr"]], axis=1)),
        "bqk": np.stack([a["L0_attn_bq"].reshape(2, P).T, a["L0_attn_bk"].reshape(2, P).T], axis=1),
        "bv": a["L0_attn_bv"].reshape(H * HD),
        "wo": chunked(a["L0_attn_Wo"]),
        "bo": a["L0_attn_bo"],
        "wgu": experts(np.concatenate([a["L0_ffn_Wg"], a["L0_ffn_Wu"]], axis=2)),
        "wd": experts(a["L0_ffn_Wd"]),
    }
    arrays = {f"in_{k}": np.ascontiguousarray(val) for k, val in arrays.items()}
    nc = bacc.Bacc("TRN2", target_bir_lowering=False, num_devices=1)
    args = {k: nc.dram_tensor(f"in_{k}", _SHAPES[k], F32, kind="ExternalInput").ap() for k in _SHAPES}
    out = nc.dram_tensor("out", (N, D), F32, kind="ExternalOutput").ap()
    build(nc, args["x"], args["wqk"], args["wvr"], args["bqk"], args["bv"], args["wo"], args["bo"], args["wgu"],
          args["wd"], out)
    r = run_bass_kernel_spmd(nc, [arrays], core_ids=[0])
    return r.results[0]["out"].reshape(B, T, D)
```

```python
from contextlib import ExitStack

import concourse.bass as bass
import numpy as np
from concourse import mybir

F32 = mybir.dt.float32
BF16 = mybir.dt.bfloat16
I32 = mybir.dt.int32
U32 = mybir.dt.uint32
ALU = mybir.AluOpType
ACT = mybir.ActivationFunctionType
AX = mybir.AxisListType

P = 128
B, T, D = 2, 1024, 256
H, HD = 16, 16
E, F = 8, 256
N = B * T
NT = N // P
TB = T // P
DC = D // P
EPS = 1e-5
SCALE = HD ** -0.5
LIMIT = 7.0
NEG = -3.0e38
BANK = 512

UH = 4
G = H // UH
UNITS = B * G
PARTS = 3
RUNS = ((0, 0, 0, 3), (3 * HD, 1, 0, 2), (5 * HD, 2, 0, 1))
MAXROW = 6 * HD
KROWS = MAXROW + PARTS
SLOTS = 3
VW = HD + 1
VROW = H * VW + 32 - VW
STEPS = [(c, j) for c in range(T // BANK) for j in range((c + 1) * BANK // P)]
NS = len(STEPS)
CHUNKS = [(h, i, s) for h in range(UH) for i in range(TB) for s in range(i * P // BANK + 1)]
NCH = len(CHUNKS)
SPS = UH + 1
SCORE_RING, NAT_RING = 2, 3
LAST_UNIT = UH * NS * (UNITS - 1)
NCH_COLS = sum(min(P * (i + 1) - BANK * s, BANK) for _, i, s in CHUNKS)
STEP_COLS = 10000
TILE_GAP = 6
QKS = B * 2 * (H * HD // P) * (T // BANK)
ZS = 6
LATE = NT - 4
MAX_TILES = 2 * N // P + E - 1
PAD = 4 * N
CONSTS = 7
NAT_EARLY = 12
QK_GAP = 3
LIST_EARLY, LIST_TO = 4, 6 * SPS
EXPERTS_FROM, EXPERTS_TO = 9 * SPS + 3, 84 * SPS
SUM_FROM = EXPERTS_TO + 8


def step_span(n):
    c, j = STEPS[n]
    t0 = max(P * j, BANK * c)
    return t0, BANK * (c + 1) - t0


def diagonal(n):
    c, j = STEPS[n]
    return P * j >= BANK * c


DIAG = [sum(diagonal(m) for m in range(n)) for n in range(NS + 1)]


def qk_tile(k):
    return k // 8, k // 4 % 2, k % 2, k // 2 % 2


def stored(k, part):
    return part if qk_tile(k)[2] else PARTS - 1 - part


def tile_starts():
    weight = {}
    for s in range(EXPERTS_FROM, EXPERTS_TO):
        width = step_span(s // SPS % NS)[1]
        natural = 4 * NCH_COLS // NCH if s // SPS < NS * (UNITS - 1) - 2 else 0
        weight[s] = max(STEP_COLS - 2 * UH * width - natural, 0)
    total, done, starts = sum(weight.values()), 0, []
    for s in weight:
        if done * MAX_TILES >= len(starts) * total and weight[s] and len(starts) < MAX_TILES:
            if not starts or s - starts[-1] >= TILE_GAP:
                starts.append(s)
        done += weight[s]
    assert len(starts) == MAX_TILES, len(starts)
    return starts


def score_bank(k):
    return k % (SCORE_RING + NAT_RING if k >= LAST_UNIT else SCORE_RING)


def make_plan():
    def qk(k):
        return [(kind, i) for i in (k, k + 1) for kind in ("qk_first", "qk")] + [("qk_lo", k), ("qk_lo", k + 1)]

    plan = [("stats", 0), ("ln", 0)] + [("xnt", 0, c) for c in range(DC)] + [("stats", 1), ("ln", 1)]
    plan += qk(0) + [("store", 0)] + [("xnt", 1, c) for c in range(DC)]
    plan += [("stats", 2)] + qk(2) + [("store", 1), ("load", 0)]
    plan += [("stats", 3), ("ln", 2), ("v", 0), ("v", 1)] + qk(4) + [("store", 2), ("ln", 3)] + qk(6)
    plan += [("store", 3), ("load", 1), ("v", 2), ("v", 3)]
    side = [("xnt", q, c) for q in range(2, 4) for c in range(DC)] + [("v", t) for t in range(4, NT)]
    side += [("top",), ("load", 2), ("route",), ("place",)]
    side += [("list", i) for i in range(LIST_EARLY)]
    for m in range(NCH):
        plan += [("nat", 0, m)]
        if m % 2 == 1 and side:
            plan += [side.pop(0)]
    plan += side + [("negate", 0), ("neg", 0)] + [("nat", 1, m) for m in range(NAT_EARLY)]

    last_slot = NS * UNITS * SPS
    beside = [[] for _ in range(last_slot)]

    def at(slot, *stages):
        beside[min(slot, last_slot - 1)].extend(stages)

    for k in range(8):
        s = k * QK_GAP
        while s // SPS % NS == 5 and s % SPS in (0, 1, 2):
            s += 1
        at(s, ("qk_first", 8 + k))
        at(s + 1, ("qk", 8 + k))
        at(s + 2, ("qk_lo", 8 + k))
        if k % 2:
            at(s + 3, ("store", 4 + k // 2))
    for k in range(8):
        at(2 * k, ("wgu", k))
        at(8 * QK_GAP + 3 + k, ("wd", k))
    at(8 * QK_GAP + 2, ("bias",))
    for t in range(NT):
        at(8 * QK_GAP + 6 + 3 * t, ("residual", t))
    for i in range(LIST_EARLY, NT):
        at((i - LIST_EARLY) * LIST_TO // (NT - LIST_EARLY), ("list", i))
    at(LIST_TO + 2, ("list_load",))
    at(LIST_TO + 6, ("token",))
    at(LIST_TO + 7, ("gather", 0), ("gather", 1))
    starts = tile_starts()
    for i, s in enumerate(starts):
        at(s, ("moe_x", i))
        if i + 2 < MAX_TILES:
            at(s, ("gather", i + 2))
        at(s + 2, ("moe_gu_first", i))
        at(s + 3, ("moe_gu", i))
        at(s + 4, ("moe_hid", i))
        at(s + 7, ("moe_h", i))
        at(s + 10, ("moe_y", i), ("scatter", i))
    taken = [s + i for s in starts for i in (2, 3)]
    for t in range(LATE):
        half_done = SPS * ((G * (t // TB) + G - 1) * NS + (6 if t % TB < 4 else NS + 2))
        s = half_done + t % 4 * (3 if t >= TB else 6)
        while s + 1 in taken:
            s += 1
        at(s, ("proj_t", t))
        at(s + 1, ("proj", t))
    for t in range(NT):
        at(SUM_FROM + t * (last_slot - SUM_FROM - 12) // NT, ("z_load", t))
        at(SUM_FROM + t * (last_slot - SUM_FROM - 12) // NT + 9, ("sum", t))
        if t < LATE:
            at(SUM_FROM + t * (last_slot - SUM_FROM - 12) // NT + 9, ("out", t))

    naturals = [("nat", u, m) for u in range(1, UNITS) for m in range(NCH)]
    lead = NS - 2
    chunk_at = [(i - NAT_EARLY) * lead * SPS // (NCH - NAT_EARLY) if i < NCH else
                SPS * (lead + (i - NCH) // 4) + (i - NCH) % 4 for i in range(len(naturals))]
    chunks = [[] for _ in range(last_slot)]
    for s, stage in list(zip(chunk_at, naturals))[NAT_EARLY:]:
        chunks[s].append(stage)

    for g in range(NS * UNITS):
        u, n = divmod(g, NS)
        half = (u, 0) if n == 5 else (u - 1, 1) if n == 1 and u else None
        for q in range(SPS):
            slot = SPS * g + q
            plan += [("s", g, q)] if q < UH else [("pv", g - 1)] if g else []
            plan += chunks[slot]
            for _, unit, m in chunks[slot]:
                if m == NCH - 1:
                    plan += [("negate", unit)]
            if q == 1 and half:
                plan += [("y_t", *half), ("norm", *half)]
            plan += beside[slot]
            if q == 0 and n == NS - 2 and u + 1 < UNITS:
                plan += [("neg", u + 1)]
            if q == 0 and n == 0 and u and u + 2 < UNITS:
                plan += [("load", u + 2)]
            if g and n in (4, 0) and q == UH:
                plan += [("y_copy", (g - 1) // NS, 0 if n == 4 else 1)]
    last = UNITS - 1
    plan += [("pv", NS * UNITS - 1), ("y_copy", last, 1), ("y_t", last, 1), ("norm", last, 1)]
    plan += [("proj_t", LATE)]
    for t in range(LATE, NT):
        plan += ([("proj_t", t + 1)] if t + 1 < NT else []) + [("proj", t), ("out", t)]
    return plan


PLAN = make_plan()


def bank_of(stage):
    kind = stage[0]
    if kind in ("xnt",):
        return stage[2] % 2
    if kind in ("qk", "v"):
        return stage[1] % 2
    if kind in ("route", "neg", "y_t", "moe_h", "moe_y", "proj_t"):
        return 0
    if kind in ("bias", "moe_x", "moe_gu", "proj"):
        return 1
    return None


FILLS = [[st for st in PLAN if bank_of(st) == bank] for bank in range(2)]
FILL_AT = {st: (bank, n) for bank in range(2) for n, st in enumerate(FILLS[bank])}


def build(nc, x_d, wqk_d, wvr_d, bqk_d, bv_d, wo_d, bo_d, wgu_d, wd_d, out_d):
    with ExitStack() as ctx:
        def sb(name, shape, dt=F32):
            return ctx.enter_context(nc.sbuf_tensor(name, shape, dt))

        def sem(name):
            return ctx.enter_context(nc.semaphore(name))

        xn_d = nc.dram_tensor("xn_rows", [N, D], F32).ap()
        qk_d = nc.dram_tensor("qk_parts", [2, 2, PARTS, HD, H // 2, N], BF16).ap()
        slot_d = nc.dram_tensor("slot_values", [MAX_TILES * P, 1], I32).ap()
        z_d = nc.dram_tensor("expert_rows", [2 * N, D], F32).ap()

        x = sb("x", [P, NT, D])
        xnt_moe = sb("xnt", [P, DC, N])
        wqk = sb("wqk", [P, 2, DC, H * HD])
        wvr = sb("wvr", [P, DC, H * HD + E])
        wo = sb("wo", [P, DC, D])
        bqk = sb("bqk", [P, 2, 2])
        bv = sb("bv", [P, DC])
        bo = sb("bo", [P, D])
        stats = sb("stats", [P, NT, 6])
        mv = sb("mv", [P, NT, 2])
        vareps = sb("vareps", [P, NT])
        rstd = sb("rstd", [P, NT])
        neghalf = sb("neghalf", [P, 4])
        stage = sb("stage", [P, 2, PARTS, T], BF16)
        resid = sb("resid", [P, 2, BANK])
        v = sb("v", [P, NT, VROW])
        packq = sb("packq", [P, SLOTS, UH, T], BF16)
        packk = sb("packk", [P, SLOTS, UH, T], BF16)
        probs = sb("probs", [P, 2, UH, BANK])
        xn = probs[:, :, :, :].rearrange("p a h n -> p (a h n)").rearrange("p (t d) -> p t d", d=D)
        maskrow = sb("maskrow", [P, BANK], BF16)
        mxa = sb("mxa", [P, 2, UH, TB])
        mxb = sb("mxb", [P, 2, UH, TB // 2])
        negm = sb("negm", [P, PARTS, UH, TB], BF16)
        negr = sb("negr", [P, UH, TB])
        negt = sb("negt", [P, P], BF16)
        yraw = sb("yraw", [P, BANK])
        rec = sb("rec", [P, 4, UH])
        y = sb("y", [P, TB, D])
        yt = sb("yt", [P, 2, DC, P])
        ident = sb("ident", [P, P])
        identb = sb("identb", [P, P], BF16)
        lower = sb("lower", [P, P], BF16)
        ones = sb("ones", [P, P], BF16)
        iota8 = sb("iota8", [P, E])
        iota128 = sb("iota128", [P, NT])
        iota_t = sb("iota_t", [P, MAX_TILES])
        slot_val = sb("slot_val", [P, NT, 2], I32)
        padv = sb("padv", [P, MAX_TILES], I32)
        lg = sb("lg", [P, NT, E])
        top = sb("top", [P, NT, E])
        topi = sb("topi", [P, NT, E], U32)
        topf = sb("topf", [P, NT, 2])
        dl = sb("dl", [P, NT])
        eg = sb("eg", [P, NT])
        gate = sb("gate", [P, NT, 2])
        hot = sb("hot", [P, 2, NT, E], BF16)
        hots = sb("hots", [P, NT, E], BF16)
        fits = sb("fits", [P, E, NT])
        ntile = sb("ntile", [P, E])
        tend = sb("tend", [P, E])
        one8 = sb("one8", [P, E])
        sbase = sb("sbase", [P, E])
        place = sb("place", [P, NT, E])
        prod = sb("prod", [P, 2, NT, E])
        posf = sb("posf", [P, 2, NT])
        posi = sb("posi", [P, 2, NT], I32)
        postile = sb("postile", [P, 2, NT], I32)
        posrow = sb("posrow", [P, 2, NT], I32)
        pos = sb("pos", [P, 2, NT], U32)
        below = sb("below", [P, MAX_TILES, E])
        eidf = sb("eidf", [P, MAX_TILES])
        eid = sb("eid", [P, MAX_TILES], I32)
        slots = sb("slots", [P, MAX_TILES], I32)
        clip = sb("clip", [P, MAX_TILES], I32)
        token = sb("token", [P, MAX_TILES], I32)
        wgu = sb("wgu", [P, E * DC * 2 * F])
        wd = xnt_moe[:, :, :].rearrange("p c n -> p (c n)")
        xg = sb("xg", [P, 2, D])
        xgt = sb("xgt", [P, 2, DC, P])
        tanh = sb("tanh", [P, 2, F])
        hid = sb("hid", [P, 2, F])
        hidt = sb("hidt", [P, 2, DC, P])
        yo = sb("yo", [P, 2, D])
        z = stage[:, :, :, :].rearrange("p a b t -> p (a b t)").bitcast(F32).rearrange("p (r k d) -> p r k d", k=2, d=D)

        ps_s = ctx.enter_context(nc.psum_tensor("ps_s", [P, SCORE_RING + NAT_RING, BANK], F32))
        ps_y = ctx.enter_context(nc.psum_tensor("ps_y", [P, BANK], F32))
        ps_w = ctx.enter_context(nc.psum_tensor("ps_w", [P, 2, BANK], F32))

        filled = [sem(f"filled{i}") for i in range(2)]
        freed = [sem(f"freed{i}") for i in range(2)]
        x_in = [sem(f"x_in{q}") for q in range(4)]
        wqk_in = sem("wqk_in")
        wvr_in = sem("wvr_in")
        wo_in = sem("wo_in")
        wgu_in = sem("wgu_in")
        wd_in = sem("wd_in")
        consts = sem("consts")
        const_step = sem("const_step")
        v_ones = sem("v_ones")
        ln_step = sem("ln_step")
        var_ready = sem("var_ready")
        rstd_ready = sem("rstd_ready")
        xn_ready = sem("xn_ready")
        xn_out = sem("xn_out")
        qk_hi = sem("qk_hi")
        qk_mid = sem("qk_mid")
        qk_lo = sem("qk_lo")
        qk_out = [sem(f"qk_out{i}") for i in range(2)]
        v_ready = sem("v_ready")
        bias_wide = sem("bias_wide")
        residual_ready = sem("residual_ready")
        pack_in = [sem(f"pack_in{i}") for i in range(SLOTS)]
        maxrow_zero = sem("maxrow_zero")
        nat_ready = sem("nat_ready")
        max_done = sem("max_done")
        neg_step = sem("neg_step")
        neg_cols = sem("neg_cols")
        neg_in = [sem(f"neg_in{i}") for i in range(SLOTS)]
        scores_ready = sem("scores_ready")
        probs_ready = sem("probs_ready")
        probs_masked = sem("probs_masked")
        pv_done = sem("pv_done")
        y_raw = sem("y_raw")
        rec_ready = sem("rec_ready")
        sum_step = sem("sum_step")
        route_step = sem("route_step")
        gate_logit = sem("gate_logit")
        gate_exp = sem("gate_exp")
        hots_ready = sem("hots_ready")
        pos_ready = sem("pos_ready")
        list_init = sem("list_init")
        list_out = sem("list_out")
        list_in = sem("list_in")
        eid_ready = sem("eid_ready")
        token_ready = sem("token_ready")
        gather_in = [sem(f"gather_in{i}") for i in range(2)]
        tanh_ready = sem("tanh_ready")
        hid_step = sem("hid_step")
        scatter_out = [sem(f"scatter_out{i}") for i in range(2)]
        z_in = [sem(f"z_in{i}") for i in range(ZS)]
        summed = sem("summed")
        out_done = sem("out_done")

        def wait_room(pe, stage):
            bank, n = FILL_AT[stage]
            if n:
                pe.wait_ge(freed[bank], n)
            return bank, filled[bank]

        def wait_filled(eng, stage):
            bank, n = FILL_AT[stage]
            eng.wait_ge(filled[bank], n + 1)
            return bank

        def wait_freed(eng, stage):
            bank, n = FILL_AT[stage]
            eng.wait_ge(freed[bank], n + 1)

        def walk(stages):
            for kind, *args in PLAN:
                if kind in stages:
                    stages[kind](*args)

        PACKS = 2 * len(RUNS)

        def span_rows(q):
            return slice(4 * q, 4 * q + 4)

        block = ctx.enter_context(nc.Block())

        @block.sync
        def _(sp):
            def store(w):
                b, grp, _, n = qk_tile(2 * w)
                sp.wait_ge(qk_hi, 2 * w + 2)
                sp.wait_ge(qk_mid, 2 * w + 2)
                sp.wait_ge(qk_lo, 2 * w + 2)
                for part in range(PARTS):
                    cols = slice(T * b + BANK * n, T * b + BANK * (n + 1))
                    sp.dma_start(qk_d[:, grp, part, :, :, cols].rearrange("o d h t -> (d h) o t"),
                                 stage[:, w % 2, part, :].rearrange("p (o t) -> p o t", o=2)).then_inc(qk_out[w % 2], 16)

            def load(u):
                b, g = divmod(u, G)
                grp, h0 = divmod(UH * g, H // 2)
                if u >= SLOTS:
                    sp.wait_ge(scores_ready, UH * NS * (u - SLOTS + 1))
                for s in qk_out:
                    sp.wait_ge(s, 16 * PARTS * (2 * b + g // 2 + 1))
                for row, *first, length in RUNS:
                    for op, pack in enumerate((packq, packk)):
                        src = qk_d[op, grp, first[op]:first[op] + length, :, h0:h0 + UH, T * b:T * b + T]
                        sp.dma_start(pack[row:row + HD * length, u % SLOTS, :, :],
                                     src.rearrange("r d h t -> (r d) h t")).then_inc(pack_in[u % SLOTS], 16)

            def neg_rows(u):
                wait_freed(sp, ("neg", u))
                for part in range(PARTS):
                    dst = packq[MAXROW + part:MAXROW + part + 1, u % SLOTS, :, :]
                    sp.dma_start(dst.rearrange("o h (i t) -> o (h i) t", t=P),
                                 negt[32 * part:32 * part + 32, :]).then_inc(neg_in[u % SLOTS], 16)

            def load_wgu(e):
                w = E * DC * 2 * F // 8
                sp.dma_start(wgu[:, w * e:w * (e + 1)], wgu_d[:, w * e:w * (e + 1)]).then_inc(wgu_in, 16)

            def load_wd(e):
                w = E * DC * D // 8
                if e == 0:
                    for k in range(QKS - 2, QKS):
                        wait_freed(sp, ("qk", k))
                    for t in range(NT - 2, NT):
                        wait_freed(sp, ("v", t))
                sp.dma_start(wd[:, w * e:w * (e + 1)], wd_d[:, w * e:w * (e + 1)]).then_inc(wd_in, 16)

            def load_list():
                sp.wait_ge(list_out, 16 * 2 * NT)
                sp.dma_start(slots[:, :], slot_d.rearrange("(p i) o -> p (i o)", p=P)).then_inc(list_in, 16)

            def load_z(t):
                if t == 0:
                    for s in range(2):
                        sp.wait_ge(scatter_out[s], 16 * len(range(s, MAX_TILES, 2)))
                    for s in qk_out:
                        sp.wait_ge(s, 16 * PARTS * QKS // 4)
                if t >= ZS:
                    sp.wait_ge(summed, t - ZS + 1)
                sp.dma_start(z[:, t % ZS, :, :],
                             z_d[2 * P * t:2 * P * (t + 1), :].rearrange("(p k) d -> p k d", k=2)).then_inc(z_in[t % ZS], 16)

            def store_out(t):
                if t < LATE:
                    sp.wait_ge(summed, t + 1)
                else:
                    wait_freed(sp, ("proj", t))
                sp.dma_start(out_d[P * t:P * (t + 1), :], x[:, t, :]).then_inc(out_done, 16)

            def store_xn(q):
                sp.wait_ge(xn_ready, 4 * (q + 1))
                sp.dma_start(xn_d[P * 4 * q:P * 4 * (q + 1), :].rearrange("(t p) d -> p t d", p=P),
                             xn[:, span_rows(q), :]).then_inc(xn_out, 16)

            for q in range(4):
                sp.dma_start(x[:, span_rows(q), :],
                             x_d[P * 4 * q:P * 4 * (q + 1), :].rearrange("(t p) d -> p t d", p=P)).then_inc(x_in[q], 16)
            sp.wait_ge(consts, 1)
            sp.dma_start(slot_d.rearrange("(p c) o -> p (c o)", p=P), padv[:, :]).then_inc(list_init, 16)
            walk({"ln": store_xn, "store": store, "load": load, "neg": neg_rows, "wgu": load_wgu, "wd": load_wd,
                  "list_load": load_list, "z_load": load_z, "out": store_out})
            sp.wait_ge(out_done, 16 * NT)

        @block.gpsimd
        def _(pool):
            steps = [0]

            def chain(ins):
                ins.then_inc(const_step, 1)
                steps[0] += 1
                pool.wait_ge(const_step, steps[0])

            def inverse_deviation(q):
                pool.wait_ge(var_ready, q + 1)
                pool.tensor_tensor(rstd[:, span_rows(q)], vareps[:, span_rows(q)], neghalf[:, :], ALU.pow)\
                    .then_inc(rstd_ready, 1)

            pool.memset(padv[:, :], PAD).then_inc(consts, 1)
            chain(pool.memset(neghalf[:, :], -0.5))
            chain(pool.memset(ident[:, :], 0.0))
            chain(pool.affine_select(out=ident[:, :], in_=ident[:, :], compare_op=ALU.not_equal, fill=1.0, base=0,
                                     pattern=[[-1, P]], channel_multiplier=1))
            pool.tensor_copy(identb[:, :], ident[:, :]).then_inc(consts, 1)
            inverse_deviation(0)
            chain(pool.memset(maskrow[:, :], 0.0))
            pool.affine_select(out=maskrow[:, BANK - P:], in_=maskrow[:, BANK - P:], compare_op=ALU.is_ge, fill=NEG,
                               base=0, pattern=[[-1, P]], channel_multiplier=1).then_inc(consts, 1)
            inverse_deviation(1)
            pool.wait_ge(rstd_ready, 2)
            chain(pool.memset(packq[MAXROW:KROWS, 0, :, :], 0.0))
            pool.memset(packk[MAXROW:KROWS, 0, :, :], 1.0).then_inc(consts, 1)
            pool.wait_ge(consts, 4)
            chain(pool.memset(lower[:, :], 0.0))
            pool.affine_select(out=lower[:, :], in_=lower[:, :], compare_op=ALU.is_ge, fill=1.0, base=0,
                               pattern=[[-1, P]], channel_multiplier=1).then_inc(consts, 1)
            inverse_deviation(2)
            pool.memset(one8[:, :], 1.0)
            pool.iota(iota8[:, :], pattern=[[1, E]], base=0, channel_multiplier=0, allow_small_or_imprecise_dtypes=True)
            pool.iota(iota128[:, :], pattern=[[P, NT]], base=0, channel_multiplier=0,
                      allow_small_or_imprecise_dtypes=True)
            inverse_deviation(3)
            pool.iota(iota_t[:, :], pattern=[[1, MAX_TILES]], base=0, channel_multiplier=0,
                      allow_small_or_imprecise_dtypes=True)
            pool.iota(slot_val[:, :, :], pattern=[[2 * P, NT], [1, 2]], base=0, channel_multiplier=2).then_inc(consts, 1)
            chain(pool.memset(ones[:, :], 1.0))
            chain(pool.memset(packq[MAXROW:KROWS, 1:, :, :], 0.0))
            pool.memset(packk[MAXROW:KROWS, 1:, :, :], 1.0).then_inc(consts, 1)

            def place_tokens(i):
                if i == 0:
                    pool.wait_ge(pos_ready, 1)
                    pool.wait_ge(list_init, 16)
                for k in range(2):
                    pool.indirect_dma_start(out=slot_d, out_offset=bass.IndirectOffsetOnAxis(ap=pos[:, k, i:i + 1], axis=0),
                                            in_=slot_val[:, i, k:k + 1], in_offset=None).then_inc(list_out, 16)

            def gather(i):
                if i == 0:
                    pool.wait_ge(token_ready, 1)
                    pool.wait_ge(xn_out, 16 * 4)
                if i >= 2:
                    wait_filled(pool, ("moe_x", i - 2))
                pool.indirect_dma_start(out=xg[:, i % 2, :], out_offset=None, in_=xn_d,
                                        in_offset=bass.IndirectOffsetOnAxis(ap=token[:, i:i + 1], axis=0))\
                    .then_inc(gather_in[i % 2], 16)

            def scatter(i):
                wait_freed(pool, ("moe_y", i))
                pool.indirect_dma_start(out=z_d, out_offset=bass.IndirectOffsetOnAxis(ap=slots[:, i:i + 1], axis=0),
                                        in_=yo[:, i % 2, :], in_offset=None, bounds_check=2 * N - 1, oob_is_err=False)\
                    .then_inc(scatter_out[i % 2], 16)

            def mask(g, h):
                u, n = divmod(g, NS)
                if h == UH - 1 and diagonal(n):
                    pool.wait_ge(probs_ready, UH * (g + 1))
                    cols = probs[:, g % 2, :, 0:P]
                    pool.affine_select(out=cols, in_=cols, compare_op=ALU.is_ge, fill=0.0, base=0,
                                       pattern=[[0, UH], [1, P]], channel_multiplier=-1).then_inc(probs_masked, 1)

            def zero_rows(u):
                if u >= SLOTS:
                    pool.wait_ge(scores_ready, UH * NS * (u - SLOTS + 1))
                    pool.wait_ge(probs_masked, DIAG[NS] * (u - 2))
                    pool.memset(packq[MAXROW:KROWS, u % SLOTS, :, :], 0.0).then_inc(maxrow_zero, 1)
                    pool.wait_ge(maxrow_zero, u - SLOTS + 1)

            walk({"list": place_tokens, "gather": gather, "scatter": scatter, "s": mask, "load": zero_rows})

        @block.scalar
        def _(act):
            def copy_xnt(q, c):
                bank = wait_filled(act, ("xnt", q, c))
                act.copy(xnt_moe[:, c, 4 * P * q:4 * P * (q + 1)], ps_w[:, bank, :]).then_inc(freed[bank], 1)

            def qk_hi_part(k):
                _, grp, op, n = qk_tile(k)
                w = k // 2
                if k == 0:
                    act.wait_ge(wqk_in, 32)
                bank = wait_filled(act, ("qk", k))
                if w >= 2:
                    act.wait_ge(qk_out[w % 2], 16 * PARTS * (w // 2))
                act.activation(stage[:, w % 2, stored(k, 0), BANK * op:BANK * (op + 1)], ps_w[:, bank, :], ACT.Identity,
                               bias=bqk[:, op, grp:grp + 1], scale=1.0).then_inc(qk_hi, 1)

            def qk_mid_part(k):
                wait_freed(act, ("qk", k))
                cols = slice(BANK * (k % 2), BANK * (k % 2 + 1))
                act.copy(stage[:, k // 2 % 2, stored(k, 1), cols], resid[:, k % 2, :]).then_inc(qk_mid, 1)

            def copy_v(t):
                if t == 0:
                    act.wait_ge(v_ones, 1)
                bank = wait_filled(act, ("v", t))
                dst = v[:, t, 0:H * VW].rearrange("p (h w) -> p h w", w=VW)[:, :, 0:HD]
                act.copy(dst, ps_w[:, bank, 0:H * HD].rearrange("p (h w) -> p h w", w=HD)).then_inc(v_ready, 1)
                act.copy(lg[:, t, :], ps_w[:, bank, H * HD:H * HD + E]).then_inc(freed[bank], 1)

            def gates():
                act.wait_ge(gate_logit, 1)
                act.activation(eg[:, :], dl[:, :], ACT.Exp).then_inc(gate_exp, 1)

            def exps(g, h):
                _, width = step_span(g % NS)
                k = UH * g + h
                act.wait_ge(scores_ready, k + 1)
                if g == 0 and h == 0:
                    act.wait_ge(xn_out, 16 * 4)
                if g >= 2 and h == 0:
                    act.wait_ge(pv_done, g - 1)
                act.activation(probs[:, g % 2, h, 0:width], ps_s[:, score_bank(k), 0:width], ACT.Exp, scale=SCALE)\
                   .then_inc(probs_ready, 1)

            def copy_y(u, c):
                act.wait_ge(pv_done, NS * u + (4 if c == 0 else NS))
                if 2 * u + c:
                    wait_filled(act, ("y_t", *divmod(2 * u + c - 1, 2)))
                act.copy(yraw[:, :], ps_y[:, :]).then_inc(y_raw, 1)

            def copy_yt(t):
                bank = wait_filled(act, ("proj_t", t))
                wait_filled(act, ("proj", t - 2) if t >= 2 else ("bias",))
                act.copy(yt[:, t % 2, :, :], ps_w[:, bank, 0:D].rearrange("p (a t) -> p a t", a=DC)).then_inc(freed[bank], 1)

            def copy_xgt(i):
                bank = wait_filled(act, ("moe_x", i))
                if i >= 2:
                    wait_filled(act, ("moe_gu", i - 2))
                act.copy(xgt[:, i % 2, :, :], ps_w[:, bank, 0:D].rearrange("p (c t) -> p c t", c=DC)).then_inc(freed[bank], 1)

            def silu_gate(i):
                bank = wait_filled(act, ("moe_gu", i))
                if i >= 2:
                    wait_freed(act, ("moe_gu", i - 2))
                act.activation(tanh[:, i % 2, :], ps_w[:, bank, 0:F], ACT.Tanh, scale=0.5).then_inc(tanh_ready, 1)

            def copy_hidt(i):
                bank = wait_filled(act, ("moe_h", i))
                if i >= 2:
                    wait_filled(act, ("moe_y", i - 2))
                act.copy(hidt[:, i % 2, :, :], ps_w[:, bank, 0:F].rearrange("p (c t) -> p c t", c=DC)).then_inc(freed[bank], 1)

            def copy_yo(i):
                bank = wait_filled(act, ("moe_y", i))
                if i >= 2:
                    act.wait_ge(scatter_out[i % 2], 16 * (i // 2))
                act.mul(yo[:, i % 2, :], ps_w[:, bank, 0:D], 0.5).then_inc(freed[bank], 1)

            act.dma_start(wqk[:, :, :, :], wqk_d).then_inc(wqk_in, 16)
            act.dma_start(bqk[:, :, :], bqk_d).then_inc(wqk_in, 16)
            act.dma_start(wvr[:, :, :], wvr_d).then_inc(wvr_in, 16)
            act.dma_start(bv[:, :], bv_d).then_inc(wvr_in, 16)
            act.dma_start(wo[:, :, :], wo_d).then_inc(wo_in, 16)
            act.dma_start(bo[:, :], bo_d.partition_broadcast(P)).then_inc(wo_in, 16)
            walk({"xnt": copy_xnt, "v": copy_v, "qk": qk_hi_part, "qk_lo": qk_mid_part, "top": gates, "s": exps,
                  "y_copy": copy_y,
                  "proj_t": copy_yt, "moe_x": copy_xgt, "moe_gu": silu_gate, "moe_h": copy_hidt, "moe_y": copy_yo})

        @block.vector
        def _(dve):
            count = {}

            def chain(s, ins):
                ins.then_inc(s, 1)
                count[s.name] = count.get(s.name, 0) + 1
                dve.wait_ge(s, count[s.name])

            def variance(q):
                dve.wait_ge(x_in[q], 16)
                for t in range(4 * q, 4 * q + 4):
                    ins = dve.bn_stats(stats[:, t, :], x[:, t, :])
                chain(ln_step, ins)
                for t in range(4 * q, 4 * q + 4):
                    ins = dve.bn_aggr(mv[:, t, :], stats[:, t, :])
                chain(ln_step, ins)
                dve.tensor_scalar(vareps[:, span_rows(q)], mv[:, span_rows(q), 1], EPS, None, ALU.add).then_inc(var_ready, 1)

            def normalise_rows(q):
                dve.wait_ge(rstd_ready, q + 1)
                for t in range(4 * q, 4 * q + 4):
                    dve.tensor_scalar(xn[:, t, :], x[:, t, :], mv[:, t, 0:1], rstd[:, t:t + 1], ALU.subtract, ALU.mult)\
                       .then_inc(xn_ready, 1)

            def qk_resid_part(k):
                _, grp, op, n = qk_tile(k)
                bank, _ = FILL_AT[("qk", k)]
                dve.wait_ge(qk_hi, k + 1)
                if k >= 2:
                    dve.wait_ge(qk_lo, k - 1)
                dve.scalar_tensor_tensor(resid[:, k % 2, :], ps_w[:, bank, :], bqk[:, op, grp:grp + 1],
                                         stage[:, k // 2 % 2, stored(k, 0), BANK * op:BANK * (op + 1)], ALU.add, ALU.subtract)\
                   .then_inc(freed[bank], 1)

            def qk_lo_part(k):
                w, op = divmod(k, 2)
                cols = slice(BANK * op, BANK * (op + 1))
                dve.wait_ge(qk_mid, k + 1)
                dve.tensor_tensor(stage[:, w % 2, stored(k, 2), cols], resid[:, k % 2, :], stage[:, w % 2, stored(k, 1), cols],
                                  ALU.subtract).then_inc(qk_lo, 1)

            def widen_v_bias():
                dve.wait_ge(wvr_in, 32)
                dve.tensor_copy(yt[:, 0, :, :], bv[:, :].unsqueeze(2).to_broadcast([P, DC, P])).then_inc(bias_wide, 1)

            def add_bias():
                bank = wait_filled(dve, ("bias",))
                dve.wait_ge(wo_in, 32)
                dve.tensor_tensor(bo[:, :], ps_w[:, bank, 0:D], bo[:, :], ALU.add).then_inc(freed[bank], 1)

            def add_bias_to_x(t):
                wait_freed(dve, ("bias",))
                dve.tensor_tensor(x[:, t, :], x[:, t, :], bo[:, :], ALU.add).then_inc(residual_ready, 1)

            def row_max(u, m):
                h, i, s = CHUNKS[m]
                n = NCH * u + m
                width = min(P * (i + 1) - BANK * s, BANK)
                into = mxa[:, u % 2, h, i:i + 1] if s == 0 else mxb[:, u % 2, h, i - TB // 2:i - TB // 2 + 1]
                chunk = ps_s[:, SCORE_RING + n % NAT_RING, 0:width]
                if n == 0:
                    dve.wait_ge(consts, 3)
                dve.wait_ge(nat_ready, n + 1)
                if s == i * P // BANK:
                    ins = dve.tensor_tensor_reduce(out=chunk, in0=chunk, in1=maskrow[:, BANK - width:], scale=1.0,
                                                   scalar=NEG, op0=ALU.add, op1=ALU.max, accum_out=into)
                else:
                    ins = dve.tensor_reduce(into, chunk, op=ALU.max, axis=AX.X)
                ins.then_inc(max_done, 1)

            def negate_max(u):
                dve.wait_ge(max_done, NCH * (u + 1))
                m = mxa[:, u % 2, :, :]
                chain(neg_step, dve.tensor_tensor(m[:, :, TB // 2:], m[:, :, TB // 2:], mxb[:, u % 2, :, :], ALU.max))
                if u:
                    wait_filled(dve, ("neg", u - 1))
                chain(neg_step, dve.tensor_scalar(negm[:, 0, :, :], m, -1.0, None, ALU.mult))
                chain(neg_step, dve.scalar_tensor_tensor(negr[:, :, :], m, -1.0, negm[:, 0, :, :], ALU.mult, ALU.subtract))
                chain(neg_step, dve.tensor_copy(negm[:, 1, :, :], negr[:, :, :]))
                dve.tensor_tensor(negm[:, 2, :, :], negr[:, :, :], negm[:, 1, :, :], ALU.subtract).then_inc(neg_cols, 1)

            def copy_neg(u):
                bank = wait_filled(dve, ("neg", u))
                if u:
                    dve.wait_ge(neg_in[(u - 1) % SLOTS], 16 * PARTS * ((u - 1) // SLOTS + 1))
                dve.tensor_copy(negt[0:96, :], ps_w[0:96, bank, 0:P // 2].bitcast(BF16)).then_inc(freed[bank], 1)

            def normalise(u, c):
                bank = wait_filled(dve, ("y_t", u, c))
                part = ps_w[:, bank, :].rearrange("p (t h w) -> p t h w", t=4, h=UH)
                chain(rec_ready, dve.reciprocal(rec[:, :, :], part[:, :, :, HD]))
                g = u % G
                if u == G:
                    wait_filled(dve, ("proj_t", 4 * c + 3))
                dst = y[:, 4 * c:4 * c + 4, UH * HD * g:UH * HD * (g + 1)].rearrange("p t (h w) -> p t h w", h=UH)
                dve.tensor_tensor(dst, part[:, :, :, 0:HD], rec[:, :, :].unsqueeze(3).to_broadcast([P, 4, UH, HD]),
                                  ALU.mult).then_inc(freed[bank], 1)

            def add_experts(t):
                dve.wait_ge(z_in[t % ZS], 16 * (t // ZS + 1))
                if t < LATE:
                    wait_freed(dve, ("proj", t))
                else:
                    dve.wait_ge(residual_ready, t + 1)
                chain(sum_step, dve.scalar_tensor_tensor(x[:, t, :], z[:, t % ZS, 0, :], gate[:, t, 0:1], x[:, t, :],
                                                         ALU.mult, ALU.add))
                dve.scalar_tensor_tensor(x[:, t, :], z[:, t % ZS, 1, :], gate[:, t, 1:2], x[:, t, :],
                                         ALU.mult, ALU.add).then_inc(summed, 1)

            def add_projection(t):
                bank = wait_filled(dve, ("proj", t))
                if t >= LATE:
                    dve.wait_ge(summed, t + 1)
                else:
                    dve.wait_ge(residual_ready, t + 1)
                dve.tensor_tensor(x[:, t, :], ps_w[:, bank, 0:D], x[:, t, :], ALU.add).then_inc(freed[bank], 1)

            def best_two():
                for t in range(NT - 2, NT):
                    wait_freed(dve, ("v", t))
                dve.wait_ge(consts, CONSTS)
                for t in range(NT):
                    ins = dve.max(top[:, t, :], lg[:, t, :])
                chain(route_step, ins)
                for t in range(NT):
                    ins = dve.max_index(topi[:, t, :], top[:, t, :], lg[:, t, :])
                dve.tensor_tensor(dl[:, :], top[:, :, 1], top[:, :, 0], ALU.subtract).then_inc(gate_logit, 1)
                chain(route_step, ins)
                chain(route_step, dve.tensor_copy(topf[:, :, :], topi[:, :, 0:2]))
                for k in range(2):
                    ins = dve.tensor_tensor(hot[:, k, :, :], iota8[:, :].unsqueeze(1).to_broadcast([P, NT, E]),
                                            topf[:, :, k:k + 1].to_broadcast([P, NT, E]), ALU.is_equal)
                chain(route_step, ins)
                dve.tensor_tensor(hots[:, :, :], hot[:, 0, :, :], hot[:, 1, :, :], ALU.add).then_inc(hots_ready, 1)

            def place_slots():
                wait_filled(dve, ("route",))
                chain(route_step, dve.tensor_tensor(fits[:, :, :], ps_w[:, 0, P:P + E].unsqueeze(2).to_broadcast([P, E, NT]),
                                                    iota128[:, :].unsqueeze(1).to_broadcast([P, E, NT]), ALU.is_gt))
                chain(route_step, dve.tensor_reduce(ntile[:, :], fits[:, :, :], op=ALU.add, axis=AX.X))
                chain(route_step, dve.tensor_tensor_scan(tend[:, :], one8[:, :], ntile[:, :], 0.0, ALU.mult, ALU.add))
                chain(route_step, dve.tensor_tensor(sbase[:, :], tend[:, :], ntile[:, :], ALU.subtract))
                chain(route_step, dve.scalar_tensor_tensor(
                    place[:, :, :], sbase[:, :].unsqueeze(1).to_broadcast([P, NT, E]), float(P),
                    ps_w[:, 0, 0:P].rearrange("p (t e) -> p t e", e=E), ALU.mult, ALU.add))
                for k in range(2):
                    ins = dve.tensor_tensor(prod[:, k, :, :], hot[:, k, :, :], place[:, :, :], ALU.mult)
                ins.then_inc(freed[0], 1)
                wait_freed(dve, ("route",))
                chain(route_step, dve.tensor_reduce(posf[:, :, :], prod[:, :, :, :], op=ALU.add, axis=AX.X))
                chain(route_step, dve.tensor_copy(posi[:, :, :], posf[:, :, :]))
                dve.tensor_scalar(postile[:, :, :], posi[:, :, :], P.bit_length() - 1, None, ALU.logical_shift_right)
                chain(route_step, dve.tensor_scalar(posrow[:, :, :], posi[:, :, :], P - 1, None, ALU.bitwise_and))
                dve.scalar_tensor_tensor(pos[:, :, :], posrow[:, :, :], float(MAX_TILES), postile[:, :, :],
                                         ALU.mult, ALU.add).then_inc(pos_ready, 1)
                chain(route_step, dve.tensor_tensor(below[:, :, :], iota_t[:, :].unsqueeze(2).to_broadcast([P, MAX_TILES, E]),
                                                    tend[:, :].unsqueeze(1).to_broadcast([P, MAX_TILES, E]), ALU.is_ge))
                chain(route_step, dve.tensor_reduce(eidf[:, :], below[:, :, :], op=ALU.add, axis=AX.X))
                dve.tensor_scalar(eid[:, :], eidf[:, :], float(E - 1), None, ALU.min).then_inc(eid_ready, 1)
                dve.wait_ge(gate_exp, 1)
                chain(route_step, dve.tensor_scalar(dl[:, :], eg[:, :], 1.0, None, ALU.add))
                chain(route_step, dve.reciprocal(gate[:, :, 0], dl[:, :]))
                chain(route_step, dve.tensor_tensor(gate[:, :, 1], gate[:, :, 0], eg[:, :], ALU.mult))

            def token_of_slot():
                dve.wait_ge(list_in, 16)
                chain(route_step, dve.tensor_scalar(clip[:, :], slots[:, :], float(2 * N - 1), None, ALU.min))
                dve.tensor_scalar(token[:, :], clip[:, :], 1, None, ALU.logical_shift_right).then_inc(token_ready, 1)

            def hidden(i):
                bank, _ = FILL_AT[("moe_gu", i)]
                dve.wait_ge(tanh_ready, i + 1)
                if i >= 2:
                    wait_filled(dve, ("moe_h", i - 2))
                chain(hid_step, dve.scalar_tensor_tensor(tanh[:, i % 2, :], tanh[:, i % 2, :], 1.0, ps_w[:, bank, 0:F],
                                                         ALU.add, ALU.mult))
                dve.scalar_tensor_tensor(hid[:, i % 2, :], tanh[:, i % 2, :], 2 * LIMIT, ps_w[:, bank, F:2 * F],
                                         ALU.min, ALU.mult).then_inc(freed[bank], 1)

            def first_constants(w):
                if w == 1:
                    dve.memset(v[:, :, 0:H * VW].rearrange("p t (h w) -> p t h w", w=VW)[:, :, :, HD:VW], 1.0)
                    dve.memset(v[:, :, H * VW:VROW], 1.0).then_inc(v_ones, 1)
                    widen_v_bias()

            walk({"stats": variance, "ln": normalise_rows, "qk": qk_resid_part, "qk_lo": qk_lo_part,
                  "store": first_constants, "top": best_two, "place": place_slots, "token": token_of_slot,
                  "bias": add_bias, "residual": add_bias_to_x, "nat": row_max, "negate": negate_max, "neg": copy_neg,
                  "norm": normalise, "moe_hid": hidden, "sum": add_experts, "proj": add_projection})

        @block.tensor
        def _(pe):
            expert = {}

            def transpose_xn(q, c):
                if q == 0 and c == 0:
                    pe.wait_ge(consts, 2)
                bank, full = wait_room(pe, ("xnt", q, c))
                pe.wait_ge(xn_ready, 4 * q + 4)
                for t in range(4):
                    ins = pe.transpose(ps_w[:, bank, P * t:P * (t + 1)], xn[:, 4 * q + t, P * c:P * (c + 1)], ident[:, :])
                ins.then_inc(full, 1)

            def qk_product(k, c):
                b, grp, op, n = qk_tile(k)
                bank, _ = FILL_AT[("qk", k)]
                cols = slice(T * b + BANK * n, T * b + BANK * (n + 1))
                return pe.matmul(ps_w[:, bank, :], wqk[:, op, c, P * grp:P * (grp + 1)], xnt_moe[:, c, cols],
                                 start=c == 0, stop=c == DC - 1)

            def project_qk_first(k):
                b, grp, op, n = qk_tile(k)
                if k == 0:
                    pe.wait_ge(wqk_in, 32)
                if grp == op == 0:
                    for c in range(DC):
                        wait_freed(pe, ("xnt", 2 * b + n, c))
                wait_room(pe, ("qk", k))
                qk_product(k, 0)

            def project_qk(k):
                qk_product(k, 1).then_inc(filled[FILL_AT[("qk", k)][0]], 1)

            def project_v(t):
                if t == 0:
                    pe.wait_ge(wvr_in, 32)
                if t == TB:
                    for c in range(DC):
                        wait_freed(pe, ("xnt", 3, c))
                bank, full = wait_room(pe, ("v", t))
                for c in range(DC):
                    ins = pe.matmul(ps_w[:, bank, 0:H * HD + E], xnt_moe[:, c, P * t:P * (t + 1)], wvr[:, c, :],
                                    start=c == 0, stop=c == DC - 1)
                ins.then_inc(full, 1)

            def route():
                pe.wait_ge(hots_ready, 1)
                bank, full = wait_room(pe, ("route",))
                pe.matmul(ps_w[:, bank, 0:P], lower[:, :], hots[:, :, :], start=True, stop=False, skip_group_check=True)
                for t in range(NT - 1):
                    left = NT - 1 - t
                    pe.matmul(ps_w[:, bank, E * (t + 1):P].rearrange("p (t e) -> p t e", e=E), ones[:, :],
                              hots[:, t:t + 1, :].to_broadcast([P, left, E]), start=False, stop=t == NT - 2,
                              skip_group_check=True)
                for t in range(NT):
                    ins = pe.matmul(ps_w[:, bank, P:P + E], ones[:, :], hots[:, t, :], start=False, stop=t == NT - 1,
                                    skip_group_check=True)
                ins.then_inc(full, 1)

            def project_bias():
                pe.wait_ge(bias_wide, 1)
                pe.wait_ge(wo_in, 32)
                bank, full = wait_room(pe, ("bias",))
                for c in range(DC):
                    ins = pe.matmul(ps_w[:, bank, 0:D], yt[:, 0, c, :], wo[:, c, :], start=c == 0, stop=c == DC - 1)
                ins.then_inc(full, 1)

            def natural(u, m):
                h, i, s = CHUNKS[m]
                n = NCH * u + m
                width = min(P * (i + 1) - BANK * s, BANK)
                if m == 0:
                    if u == 0:
                        pe.wait_ge(consts, 4)
                    elif u == 1:
                        pe.wait_ge(consts, CONSTS)
                    pe.wait_ge(pack_in[u % SLOTS], 16 * PACKS * (u // SLOTS + 1))
                    if u >= SLOTS:
                        pe.wait_ge(maxrow_zero, u - SLOTS + 1)
                if n >= NAT_RING:
                    pe.wait_ge(max_done, n - NAT_RING + 1)
                pe.matmul(ps_s[:, SCORE_RING + n % NAT_RING, 0:width], packq[0:KROWS, u % SLOTS, h, P * i:P * (i + 1)],
                          packk[0:KROWS, u % SLOTS, h, BANK * s:BANK * s + width], start=True, stop=True)\
                  .then_inc(nat_ready, 1)

            def transpose_neg(u):
                pe.wait_ge(neg_cols, u + 1)
                bank, full = wait_room(pe, ("neg", u))
                pe.transpose(ps_w[0:96, bank, 0:P // 2].bitcast(BF16), negm[:, :, :, :].rearrange("p a h i -> p (a h i)"),
                             identb[:, :]).then_inc(full, 1)

            def scores(g, h):
                u, n = divmod(g, NS)
                t0, width = step_span(n)
                j = STEPS[n][1]
                k = UH * g + h
                if n == 0 and h == 0:
                    pe.wait_ge(neg_in[u % SLOTS], 16 * PARTS * (u // SLOTS + 1))
                before = [m for m in range(k) if score_bank(m) == score_bank(k)]
                if before:
                    pe.wait_ge(probs_ready, before[-1] + 1)
                elif k >= LAST_UNIT:
                    pe.wait_ge(max_done, NCH * UNITS)
                pe.matmul(ps_s[:, score_bank(k), 0:width], packk[0:KROWS, u % SLOTS, h, P * j:P * (j + 1)],
                          packq[0:KROWS, u % SLOTS, h, t0:t0 + width], start=True, stop=True).then_inc(scores_ready, 1)

            def weigh_v(g):
                u, n = divmod(g, NS)
                c, j = STEPS[n]
                t0, width = step_span(n)
                b, gr = divmod(u, G)
                if g == 0:
                    pe.wait_ge(v_ready, NT)
                pe.wait_ge(probs_ready, UH * (g + 1))
                if diagonal(n):
                    pe.wait_ge(probs_masked, DIAG[NS] * u + DIAG[n + 1])
                if j == 0 and 2 * u + c:
                    pe.wait_ge(y_raw, 2 * u + c)
                last = (c + 1) * BANK // P - 1
                for h in range(UH):
                    at = VW * (UH * gr + h)
                    ins = pe.matmul(ps_y[32 * h:32 * h + 32, t0 - BANK * c:BANK], v[:, TB * b + j, at:at + 32],
                                    probs[:, g % 2, h, 0:width], start=j == 0, stop=j == last, skip_group_check=True)
                ins.then_inc(pv_done, 1)

            def transpose_y(u, c):
                pe.wait_ge(y_raw, 2 * u + c + 1)
                bank, full = wait_room(pe, ("y_t", u, c))
                for t in range(4):
                    ins = pe.transpose(ps_w[:, bank, P * t:P * (t + 1)], yraw[:, P * t:P * (t + 1)], ident[:, :])
                ins.then_inc(full, 1)

            def transpose_heads(t):
                if t % 4 == 0:
                    wait_freed(pe, ("y_t", G * (t // TB) + G - 1, t // 4 % 2))
                bank, full = wait_room(pe, ("proj_t", t))
                for c in range(DC):
                    ins = pe.transpose(ps_w[:, bank, P * c:P * (c + 1)], y[:, t % TB, P * c:P * (c + 1)], ident[:, :])
                ins.then_inc(full, 1)

            def project(t):
                if t == 0:
                    pe.wait_ge(wo_in, 32)
                wait_freed(pe, ("proj_t", t))
                bank, full = wait_room(pe, ("proj", t))
                for c in range(DC):
                    ins = pe.matmul(ps_w[:, bank, 0:D], yt[:, t % 2, c, :], wo[:, c, :], start=c == 0, stop=c == DC - 1)
                ins.then_inc(full, 1)

            def transpose_rows(i):
                pe.wait_ge(gather_in[i % 2], 16 * (i // 2 + 1))
                bank, full = wait_room(pe, ("moe_x", i))
                for c in range(DC):
                    ins = pe.transpose(ps_w[:, bank, P * c:P * (c + 1)], xg[:, i % 2, P * c:P * (c + 1)], ident[:, :])
                ins.then_inc(full, 1)

            def gu_product(i, c):
                bank, _ = FILL_AT[("moe_gu", i)]
                return pe.matmul(ps_w[:, bank, :], xgt[:, i % 2, c, :],
                                 wgu[:, bass.ds(expert[i] * (DC * 2 * F) + c * 2 * F, 2 * F)],
                                 start=c == 0, stop=c == DC - 1)

            def gate_up_first(i):
                if i == 0:
                    pe.wait_ge(eid_ready, 1)
                    pe.wait_ge(wgu_in, 16 * 8)
                    pe.wait_ge(wd_in, 16 * 8)
                expert[i] = pe.value_load(eid[0:1, i:i + 1], min_val=0, max_val=E - 1)
                wait_freed(pe, ("moe_x", i))
                wait_room(pe, ("moe_gu", i))
                gu_product(i, 0)

            def gate_up(i):
                gu_product(i, 1).then_inc(filled[FILL_AT[("moe_gu", i)][0]], 1)

            def transpose_hidden(i):
                wait_freed(pe, ("moe_gu", i))
                bank, full = wait_room(pe, ("moe_h", i))
                for c in range(DC):
                    ins = pe.transpose(ps_w[:, bank, P * c:P * (c + 1)], hid[:, i % 2, P * c:P * (c + 1)], ident[:, :])
                ins.then_inc(full, 1)

            def down(i):
                wait_freed(pe, ("moe_h", i))
                bank, full = wait_room(pe, ("moe_y", i))
                for c in range(DC):
                    ins = pe.matmul(ps_w[:, bank, 0:D], hidt[:, i % 2, c, :],
                                    wd[:, bass.ds(expert[i] * (DC * D) + c * D, D)], start=c == 0, stop=c == DC - 1)
                ins.then_inc(full, 1)

            walk({"xnt": transpose_xn, "qk_first": project_qk_first, "qk": project_qk, "v": project_v, "route": route,
                  "bias": project_bias, "nat": natural,
                  "neg": transpose_neg, "s": scores, "pv": weigh_v, "y_t": transpose_y, "proj_t": transpose_heads,
                  "proj": project, "moe_x": transpose_rows, "moe_gu_first": gate_up_first, "moe_gu": gate_up,
                  "moe_h": transpose_hidden,
                  "moe_y": down})


_SHAPES = {
    "x": (N, D), "wqk": (P, 2, DC, H * HD), "wvr": (P, DC, H * HD + E), "bqk": (P, 2, 2), "bv": (P, DC),
    "wo": (P, DC, D), "bo": (D,), "wgu": (P, E * DC * 2 * F), "wd": (P, E * DC * D),
}


def kernel(**inputs):
    import concourse.bacc as bacc
    from concourse.bass_utils import run_bass_kernel_spmd

    a = {k: np.asarray(val) for k, val in inputs.items()}

    def chunked(w):
        return w.reshape(-1, P, w.shape[-1]).transpose(1, 0, 2)

    def heads(w):
        return w.transpose(1, 0, 2).reshape(D, H * HD)

    def groups(w):
        return np.moveaxis(w.reshape(2, H // 2, -1, HD), (2, 0, 3, 1), (0, 1, 2, 3)).reshape(-1, H * HD)

    def experts(w):
        return np.stack([chunked(m) for m in w], axis=1).reshape(P, -1)

    arrays = {
        "x": a["L0_attn_x"].reshape(N, D),
        "wqk": np.stack([chunked(groups(a["L0_attn_Wq"])), chunked(groups(a["L0_attn_Wk"]))], axis=1),
        "wvr": chunked(np.concatenate([heads(a["L0_attn_Wv"]), a["L0_ffn_Wr"]], axis=1)),
        "bqk": np.stack([groups(a["L0_attn_bq"]).reshape(2, P).T, groups(a["L0_attn_bk"]).reshape(2, P).T], axis=1),
        "bv": a["L0_attn_bv"].reshape(DC, P).T,
        "wo": chunked(a["L0_attn_Wo"]),
        "bo": a["L0_attn_bo"],
        "wgu": experts(np.concatenate([a["L0_ffn_Wg"], a["L0_ffn_Wu"]], axis=2)),
        "wd": experts(a["L0_ffn_Wd"]),
    }
    arrays = {f"in_{k}": np.ascontiguousarray(val) for k, val in arrays.items()}
    nc = bacc.Bacc("TRN2", target_bir_lowering=False, num_devices=1)
    args = {k: nc.dram_tensor(f"in_{k}", _SHAPES[k], F32, kind="ExternalInput").ap() for k in _SHAPES}
    out = nc.dram_tensor("out", (N, D), F32, kind="ExternalOutput").ap()
    build(nc, args["x"], args["wqk"], args["wvr"], args["bqk"], args["bv"], args["wo"], args["bo"], args["wgu"],
          args["wd"], out)
    r = run_bass_kernel_spmd(nc, [arrays], core_ids=[0])
    return r.results[0]["out"].reshape(B, T, D)
```
